# Optimizing a Trainium2 kernel written in Bass

```python
import numpy as np
import jax
import jax.numpy as jnp

def _softmax(x, axis=-1):
    return jax.nn.softmax(x, axis=axis)

def _gelu(x):
    return jax.nn.gelu(x, approximate=True)

def _silu(x):
    return jax.nn.silu(x)

def _sigmoid(x):
    return jax.nn.sigmoid(x)

def _layernorm(x, axis=-1, eps=1e-05):
    m = jnp.mean(x, axis=axis, keepdims=True)
    v = jnp.var(x, axis=axis, keepdims=True)
    return (x - m) / jnp.sqrt(v + eps)

def _scatter_add(tgt, idx, src, axis=0):
    return tgt.at[idx].add(src)

def _segment_sum(src, seg, n):
    return jax.ops.segment_sum(src, seg, n)
kernel_name = 'mk_lm_tower_d1_tok_ids256_r4_f806d3'

def setup_inputs(seed: int=0):
    np.random.seed(seed)
    _w = jnp.asarray

    def _rec_inputs():
        import jax
        import jax.numpy as jnp
        _rk = jax.random.key(seed)
        x = jax.random.randint(jax.random.fold_in(_rk, 1), (8, 512), 0, 50257, jnp.int32)
        return x
    x = _rec_inputs()

    def _L0_tok_setup():
        import jax, jax.numpy as jnp
        import numpy as np
        VOCAB = 50257
        DIM = 64

        def _positional_table(seq_len, dim, dtype=jnp.float32):
            pos = jnp.arange(seq_len, dtype=dtype)[:, None]
            d = jnp.arange(dim)
            exponent = (d - d % 2).astype(dtype) / dim
            inv_freq = jnp.power(jnp.asarray(10000.0, dtype), -exponent)
            angle = pos * inv_freq
            return jnp.where(d % 2 == 0, jnp.sin(angle), jnp.cos(angle))
        key = jax.random.key(seed)
        k1, k2 = jax.random.split(key)
        x = jax.random.randint(k1, (32, 1024), 0, VOCAB)
        W = jax.random.normal(k2, (VOCAB, DIM), dtype=jnp.float32)
        return {'x': x, 'W': W}
    _L0_tok_all = _L0_tok_setup()
    _L0_tok_in = {k: v for k, v in _L0_tok_all.items() if k in ('W',)}
    del _L0_tok_all

    def _L0_attn_setup():
        import jax, jax.numpy as jnp
        import numpy as np
        D_MODEL = 64
        key = jax.random.key(seed)
        k_x, k_wqkv, k_bqkv, k_wp, k_bp = jax.random.split(key, 5)
        B, T, d = (4, 1024, D_MODEL)
        bound_qkv = 1.0 / np.sqrt(d)
        return {'x': jax.random.normal(k_x, (B, T, d), dtype=jnp.float32), 'W_qkv': jax.random.uniform(k_wqkv, (d, 3 * d), jnp.float32, -bound_qkv, bound_qkv), 'b_qkv': jax.random.uniform(k_bqkv, (3 * d,), jnp.float32, -bound_qkv, bound_qkv), 'W_proj': jax.random.uniform(k_wp, (d, d), jnp.float32, -bound_qkv, bound_qkv), 'b_proj': jax.random.uniform(k_bp, (d,), jnp.float32, -bound_qkv, bound_qkv)}
    _L0_attn_all = _L0_attn_setup()
    _L0_attn_in = {k: v for k, v in _L0_attn_all.items() if k in ('W_qkv', 'b_qkv', 'W_proj', 'b_proj')}
    del _L0_attn_all

    def _L0_ffn_setup():
        import jax, jax.numpy as jnp
        import numpy as np
        NUM_EXPERTS = 8
        TOP_K = 2
        B, S, D = (8, 2048, 64)

        def _moe(tokens, router_w, w1, b1, w2, b2):
            N = tokens.shape[0]
            E = router_w.shape[0]
            logits = tokens.astype(jnp.float32) @ router_w.astype(jnp.float32).T
            probs = jax.nn.softmax(logits, axis=-1)
            rw, re = jax.lax.top_k(probs, TOP_K)
            if TOP_K > 1:
                rw = rw / jnp.maximum(rw.sum(-1, keepdims=True), 1e-12)
            rw = rw.astype(tokens.dtype)
            combine = jnp.zeros((N, E), tokens.dtype).at[jnp.arange(N)[:, None], re].set(rw)
            out = tokens
            for e in range(E):
                h = jax.nn.gelu(tokens @ w1[e] + b1[e], approximate=False)
                y = h @ w2[e] + b2[e]
                out = out + combine[:, e:e + 1] * y
            return out
        key = jax.random.key(seed)
        ks = jax.random.split(key, 4)
        scale = 1.0 / np.sqrt(D).astype(np.float32)
        return {'input_embeddings': jax.random.normal(ks[0], (B, S, D), jnp.float32), 'router_w': jax.random.normal(ks[1], (NUM_EXPERTS, D), jnp.float32) * scale, 'w1': jax.random.normal(ks[2], (NUM_EXPERTS, D, D), jnp.float32) * scale, 'b1': jnp.zeros((NUM_EXPERTS, D), jnp.float32), 'w2': jax.random.normal(ks[3], (NUM_EXPERTS, D, D), jnp.float32) * scale, 'b2': jnp.zeros((NUM_EXPERTS, D), jnp.float32)}
    _L0_ffn_all = _L0_ffn_setup()
    _L0_ffn_in = {k: v for k, v in _L0_ffn_all.items() if k in ('router_w', 'w1', 'b1', 'w2', 'b2')}
    del _L0_ffn_all
    return {'x': x, 'L0_tok_W': _L0_tok_in['W'], 'L0_attn_W_qkv': _L0_attn_in['W_qkv'], 'L0_attn_b_qkv': _L0_attn_in['b_qkv'], 'L0_attn_W_proj': _L0_attn_in['W_proj'], 'L0_attn_b_proj': _L0_attn_in['b_proj'], 'L0_ffn_router_w': _L0_ffn_in['router_w'], 'L0_ffn_w1': _L0_ffn_in['w1'], 'L0_ffn_b1': _L0_ffn_in['b1'], 'L0_ffn_w2': _L0_ffn_in['w2'], 'L0_ffn_b2': _L0_ffn_in['b2']}

def reference(x, L0_tok_W, L0_attn_W_qkv, L0_attn_b_qkv, L0_attn_W_proj, L0_attn_b_proj, L0_ffn_router_w, L0_ffn_w1, L0_ffn_b1, L0_ffn_w2, L0_ffn_b2):
    import jax
    import jax.numpy as jnp

    def _L0_tok_ref(x, W):
        import jax, jax.numpy as jnp
        import numpy as np
        VOCAB = 50257
        DIM = 64

        def _positional_table(seq_len, dim, dtype=jnp.float32):
            pos = jnp.arange(seq_len, dtype=dtype)[:, None]
            d = jnp.arange(dim)
            exponent = (d - d % 2).astype(dtype) / dim
            inv_freq = jnp.power(jnp.asarray(10000.0, dtype), -exponent)
            angle = pos * inv_freq
            return jnp.where(d % 2 == 0, jnp.sin(angle), jnp.cos(angle))
        seq_len = x.shape[1]
        pe = _positional_table(seq_len, W.shape[1], W.dtype)
        return W[x] + pe[None, :, :]

    def _L0_attn_ref(x, W_qkv, b_qkv, W_proj, b_proj):
        import jax, jax.numpy as jnp
        import numpy as np
        D_MODEL = 64
        B, T, d = x.shape
        qkv = x @ W_qkv + b_qkv
        q, k, v = jnp.split(qkv, 3, axis=-1)
        scale = 1.0 / np.sqrt(d).astype(np.float32)
        scores = jnp.einsum('btd,bsd->bts', q, k) * scale
        causal = jnp.tril(jnp.ones((T, T), dtype=bool))
        scores = jnp.where(causal, scores, -jnp.inf)
        weights = jax.nn.softmax(scores, axis=-1)
        ctx = jnp.einsum('bts,bsd->btd', weights, v)
        return ctx @ W_proj + b_proj

    def _L0_ffn_ref(input_embeddings, router_w, w1, b1, w2, b2):
        import jax, jax.numpy as jnp
        import numpy as np
        NUM_EXPERTS = 8
        TOP_K = 2
        B, S, D = (8, 2048, 64)

        def _moe(tokens, router_w, w1, b1, w2, b2):
            N = tokens.shape[0]
            E = router_w.shape[0]
            logits = tokens.astype(jnp.float32) @ router_w.astype(jnp.float32).T
            probs = jax.nn.softmax(logits, axis=-1)
            rw, re = jax.lax.top_k(probs, TOP_K)
            if TOP_K > 1:
                rw = rw / jnp.maximum(rw.sum(-1, keepdims=True), 1e-12)
            rw = rw.astype(tokens.dtype)
            combine = jnp.zeros((N, E), tokens.dtype).at[jnp.arange(N)[:, None], re].set(rw)
            out = tokens
            for e in range(E):
                h = jax.nn.gelu(tokens @ w1[e] + b1[e], approximate=False)
                y = h @ w2[e] + b2[e]
                out = out + combine[:, e:e + 1] * y
            return out
        b, s, d = input_embeddings.shape
        tokens = input_embeddings.reshape(b * s, d)
        return _moe(tokens, router_w, w1, b1, w2, b2).reshape(b, s, d)
    h = _L0_tok_ref(x, L0_tok_W)
    h = h + _L0_attn_ref(_layernorm(h, axis=-1), L0_attn_W_qkv, L0_attn_b_qkv, L0_attn_W_proj, L0_attn_b_proj)
    h = h + _L0_ffn_ref(_layernorm(h, axis=-1), L0_ffn_router_w, L0_ffn_w1, L0_ffn_b1, L0_ffn_w2, L0_ffn_b2)
    return h

_drawn_inputs = setup_inputs


def setup_inputs(seed=0):
    import zlib

    import numpy as np

    out = dict(_drawn_inputs(seed))
    spreads = {'L0_ffn_b1': (0.0, 0.365), 'L0_ffn_b2': (0.0, 0.1)}
    factors = {}
    for name, (base, spread) in spreads.items():
        noise = np.random.default_rng([zlib.crc32(name.encode()), seed]).standard_normal(out[name].shape)
        drawn = base * np.exp(spread * noise) if base else spread * noise
        out[name] = jnp.asarray(drawn.astype(out[name].dtype))
    for name, factor in factors.items():
        out[name] = (out[name] * factor).astype(out[name].dtype)
    return out
```

```python
from contextlib import ExitStack

import numpy as np
import concourse.bass as bass
from concourse import mybir

F32 = mybir.dt.float32
F32R = mybir.dt.float32r
BF16 = mybir.dt.bfloat16
U32 = mybir.dt.uint32
I32 = mybir.dt.int32
ALU = mybir.AluOpType
ACT = mybir.ActivationFunctionType
AXX = mybir.AxisListType.X

B, T, D = 8, 512, 64
E, TOPK = 8, 2
P = 128
Q = T // P
PAIRS = E * D // P
VW = D + 2
SPLIT = 3
KC = SPLIT * E
KG = 32
KB = SPLIT * KG
EPS = 1e-5
SCALE = float(D) ** -0.5
GUARD = 1e-12
MASKED = -1e30

C_ID, C_PE, C_IOTA, C_F32 = 0, P, P + Q * D, P + Q * D + E
C_MASK, C_SEL, C_BF16 = P, 2 * P, 2 * P + PAIRS * P


class Steps:

    def __init__(self, sem, per=1):
        self.sem, self.per = sem, per

    def at(self, batch, step=None):
        return batch * self.per + (self.per if step is None else step)


def build(nc, ids, table, w_qkv, b_qkv, w_proj, b_proj, router, w1, b1, w2, b2, const, const_b, out):
    ctx = ExitStack()
    with ctx:
        def sb(name, shape, dt=F32):
            return ctx.enter_context(nc.sbuf_tensor(name, shape, dt))

        def bank(name):
            return ctx.enter_context(nc.psum_tensor(name, [P, 512], F32))

        def sem(name):
            return ctx.enter_context(nc.semaphore(name))

        def steps(name, per=1):
            return Steps(sem(name), per)

        cf = sb("cf", [P, C_F32])
        cb_f = sb("cb_f", [P, C_BF16])
        cb = sb("cb", [P, C_BF16], BF16)
        ident = cf[:, C_ID:C_ID + P]
        pos = cf[:, C_PE:C_PE + Q * D].rearrange("p (q d) -> p q d", q=Q)
        iota = cf[:, C_IOTA:C_IOTA + E]
        ident_b = cb[:, C_ID:C_ID + P]
        mask = cb[:, C_MASK:C_MASK + P]
        select = cb[:, C_SEL:C_SEL + PAIRS * P].rearrange("k (a m) -> k a m", a=PAIRS)
        idx = sb("idx", [P, B * Q], I32)
        idx_v = idx[:, :].rearrange("p (b q) -> p b q", q=Q)
        ids_now = sb("ids_now", [P, Q], I32)
        rows = sb("rows", [P, Q, D])
        wqkv = sb("wqkv", [D, 3 * D])
        bcol = sb("bcol", [D, 3])
        wp = sb("wp", [D, D])
        bp = sb("bp", [P, D])
        wT = sb("wT", [D, 3, 2, D])
        bq_rows = sb("bq_rows", [D, P])
        bv_rows = sb("bv_rows", [D, P])
        a_hi, a_lo = sb("a_hi", [P, P], F32R), sb("a_lo", [P, P], F32R)
        c_col = sb("c_col", [P, 1])
        wv_f = sb("wv_f", [P, VW])
        wv_hi, wv_lo = sb("wv_hi", [P, VW], F32R), sb("wv_lo", [P, VW], F32R)
        v_bias = sb("v_bias", [P, VW])
        r_f = sb("r_f", [P, E])
        r_hi, r_lo = sb("r_hi", [P, E], F32R), sb("r_lo", [P, E], F32R)
        w1_f = sb("w1_f", [P, E * D])
        w1_hi, w1_lo = sb("w1_hi", [P, E * D], F32R), sb("w1_lo", [P, E * D], F32R)
        b1_col = sb("b1_col", [P, PAIRS])
        w2_sb = sb("w2_sb", [P, PAIRS, D])
        b2_f = sb("b2_f", [KB, D])
        b2_rest = sb("b2_rest", [KB, 2, D])
        b2_part = sb("b2_part", [KB, SPLIT, D], BF16)
        b2_rows = sb("b2_rows", [KB, D], BF16)
        powers = sb("powers", [P, Q + 1])

        stream = sb("stream", [P, B, Q, D])
        ln = []
        for k in (1, 2):
            ln.append(dict(
                stats=sb(f"stats{k}", [P, Q, 6]), diff=sb(f"diff{k}", [P, Q]), both=sb(f"both{k}", [P, Q, 2]),
                between=sb(f"between{k}", [P, Q]), within=sb(f"within{k}", [P, Q]), mean=sb(f"mean{k}", [P, Q]),
                var=sb(f"var{k}", [P, Q]), rstd=sb(f"rstd{k}", [P, Q]), xn=sb(f"xn{k}", [P, Q, D]), xs=sb(f"xs{k}", [P, Q, 2, D])))
        xT = sb("xT", [P, T], F32R)
        x2T = sb("x2T", [P, T], F32R)
        g_hi, g_lo = sb("g_hi", [P, T], F32R), sb("g_lo", [P, T], F32R)
        v_sb = sb("v_sb", [P, Q, VW])
        row_max = sb("row_max", [P, Q])
        shift = sb("shift", [P, Q])
        probs = sb("probs", [P, Q, T])
        row_sum = sb("row_sum", [P, Q])
        row_inv = sb("row_inv", [P, Q])
        pT = sb("pT", [P, Q, Q, P])
        top = sb("top", [P, Q, E])
        top_i = sb("top_i", [P, Q, E], U32)
        top_d = sb("top_d", [P, Q, E])
        top_e = sb("top_e", [P, Q, E])
        chosen = sb("chosen", [P, Q, TOPK, E])
        esum = sb("esum", [P, Q, 1])
        pair_sum = sb("pair_sum", [P, Q, 1])
        denom = sb("denom", [P, Q, 1])
        inv = sb("inv", [P, Q, 1])
        weight = sb("weight", [P, Q, TOPK])
        placed = sb("placed", [P, Q, TOPK, E])
        comb = sb("comb", [P, Q, E])
        comb_rest = sb("comb_rest", [P, Q, E])
        comb_part = sb("comb_part", [P, Q, SPLIT, KG], BF16)
        cT = sb("cT", [KB, T], BF16)
        hg = sb("hg", [P, 2, T])
        hs = sb("hs", [P, PAIRS, T])
        yT = sb("yT", [D, T])

        bT = bank("bT")
        bG = bank("bG")
        bM = bank("bM")
        bS = [bank("bS0"), bank("bS1")]
        bX = bank("bX")
        bO = bank("bO")
        bY = bank("bY")
        v_ps = bM[:, 0:Q * VW].rearrange("p (q n) -> p q n", q=Q)
        l_ps = bM[:, Q * VW:Q * VW + Q * E].rearrange("p (q e) -> p q e", q=Q)
        ct_ps = bM[:, 0:T // 2].bitcast(BF16)
        o_ps = bO[:, 0:Q * D].rearrange("p (q d) -> p q d", q=Q)
        y_ps = bY[:, 0:Q * D].rearrange("p (q d) -> p q d", q=Q)
        w_bank = [bX, bG]

        s_idx, s_cf, s_cbf, s_cb = sem("s_idx"), sem("s_cf"), sem("s_cbf"), sem("s_cb")
        s_attw, s_wp, s_moew = sem("s_attw"), sem("s_wp"), sem("s_moew")
        s_half = sem("s_half")
        s_zeroed = sem("s_zeroed")
        s_wt_ps, s_wt, s_ab_ps = sem("s_wt_ps"), sem("s_wt"), sem("s_ab_ps")
        s_prep = sem("s_prep")
        s_w1hi = sem("s_w1hi")
        picked = steps("picked")
        gathered = steps("gathered", 16 * Q)
        embedded = steps("embedded")
        ln_dve = [steps("ln1_dve", 5), steps("ln2_dve", 5)]
        ln_pool = [steps("ln1_pool", 3), steps("ln2_pool", 3)]
        resid = steps("resid")
        xT_ps, xT_sb = steps("xT_ps"), steps("xT_sb")
        x2T_ps, x2T_sb = steps("x2T_ps"), steps("x2T_sb")
        g_ps, g_hi_sb, g_lo_sb = steps("g_ps"), steps("g_hi_sb"), steps("g_lo_sb")
        v_done, v_ready = steps("v_done"), steps("v_ready")
        scored = steps("scored", Q)
        maxed = steps("maxed", Q)
        shifted = steps("shifted", Q)
        exped = steps("exped", Q)
        turned = steps("turned", Q)
        pT_dve, pT_act = steps("pT_dve", 2), steps("pT_act", 2)
        attended = steps("attended", Q)
        inverted = steps("inverted")
        added = steps("added")
        routed_ps = steps("routed_ps")
        route = steps("route", 15)
        route_exp = steps("route_exp")
        ct_done, ct_ready = steps("ct_done"), steps("ct_ready")
        hidden = steps("hidden", PAIRS)
        spread = steps("spread", PAIRS)
        gelued = steps("gelued", PAIRS)
        scaled = steps("scaled", PAIRS)
        mixed = steps("mixed")
        yT_sb = steps("yT_sb")
        unmixed = steps("unmixed")
        finished = steps("finished")
        s_store = sem("s_store")

        (PREP_BQ, PREP_BV, PREP_C, PREP_AHI, PREP_ALO, PREP_WV, PREP_WU, PREP_WPAD, PREP_VB, PREP_VK, PREP_VPAD,
         PREP_WVHI, PREP_WVLO, PREP_RHI, PREP_RLO, PREP_W1LO, PREP_B2) = range(1, 18)
        PREP_ALL = PREP_B2 + 3 * SPLIT - 2

        def has(batch):
            return not isinstance(batch, int) or 0 <= batch < B

        def peeled(i, n):
            return isinstance(i, int) and i == n

        def constant_wait(eng):
            eng.wait_ge(s_idx, 16)

        def pipeline(eng, body):
            for i in (0, 1):
                body(i)
            with eng.Fori(2, B - 1) as i:
                body(i)
            for i in (B - 1, B, B + 1):
                body(i)

        block = ctx.enter_context(nc.Block())

        @block.sync
        def _(sp):
            sp.dma_start(idx[:, :], ids).then_inc(s_idx, 16)
            sp.dma_start(cf[:, :], const).then_inc(s_cf, 16)
            sp.dma_start(wp[:, :], w_proj).then_inc(s_wp, 16)
            sp.dma_start(bp[:, :], b_proj.partition_broadcast(P)).then_inc(s_wp, 16)
            for half in range(2):
                rows = slice(half * D, half * D + D)
                sp.dma_start(w1_f[rows, :].rearrange("i (e f) -> i e f", e=E),
                             w1.rearrange("e i f -> i e f")).then_inc(s_moew, 16)
                sp.dma_start(r_f[rows, :], router).then_inc(s_moew, 16)
            sp.dma_start(w2_sb[:, :, :], w2.rearrange("(a e) f d -> (e f) a d", e=2)).then_inc(s_moew, 16)
            sp.dma_start(b1_col[:, :], b1).then_inc(s_moew, 16)
            sp.wait_ge(s_zeroed, 2)
            for part in range(SPLIT):
                for copy in range(SPLIT):
                    at = copy * KG + part * E
                    sp.dma_start(b2_f[at:at + E, :], b2).then_inc(s_moew, 16)

            out_v = out.rearrange("b (q p) d -> b p q d", q=Q)
            with sp.Fori(0, B) as b:
                sp.wait_ge(finished.sem, finished.at(b))
                sp.dma_start(out_v[b], stream[:, b]).then_inc(s_store, 16)
            sp.wait_ge(s_store, 16 * B)

        @block.gpsimd
        def _(pool):
            def pick(b):
                pool.tensor_copy(ids_now[:, :], idx_v[:, b, :]).then_inc(picked.sem, 1)

            def gather(b):
                for q in range(Q):
                    pool.indirect_dma_start(
                        out=rows[:, q, :], out_offset=None, in_=table,
                        in_offset=bass.IndirectOffsetOnAxis(ap=ids_now[:, q:q + 1], axis=0),
                        bounds_check=table.shape[0] - 1).then_inc(gathered.sem, 16)

            def embed(b):
                pool.wait_ge(gathered.sem, gathered.at(b))
                pool.tensor_tensor(stream[:, b], rows[:, :, :], pos, ALU.add).then_inc(embedded.sem, 1)

            def inverse_deviation(k, b):
                n, mine, dve = ln[k], ln_pool[k], ln_dve[k]
                pool.wait_ge(dve.sem, dve.at(b, 4))
                pool.tensor_tensor(n["rstd"][:, :], n["var"][:, :], powers[:, 0:Q], ALU.pow).then_inc(mine.sem, 1)

            def split(k, b, read):
                n, mine, dve = ln[k], ln_pool[k], ln_dve[k]
                pool.wait_ge(dve.sem, dve.at(b, 5))
                if has(b - 1):
                    pool.wait_ge(read.sem, read.at(b - 1))
                pool.tensor_tensor(n["xs"][:, :, 0, :].bitcast(F32R), n["xn"][:, :, :],
                                   powers[:, Q:Q + 1].unsqueeze(2).to_broadcast([P, Q, D]), ALU.add)\
                    .then_inc(mine.sem, 1)
                pool.wait_ge(mine.sem, mine.at(b, 2))
                pool.tensor_tensor(n["xs"][:, :, 1, :], n["xn"][:, :, :], n["xs"][:, :, 0, :], ALU.subtract)\
                    .then_inc(mine.sem, 1)

            def norm1(b):
                if has(b):
                    inverse_deviation(0, b)
                    split(0, b, xT_ps)

            def norm2(b):
                if has(b):
                    inverse_deviation(1, b)
                    split(1, b, x2T_ps)
                    pool.tensor_tensor(stream[:, b], stream[:, b], ln[1]["xn"][:, :, :], ALU.add)\
                        .then_inc(resid.sem, 1)

            pool.memset(powers[:, 0:Q], -0.5).then_inc(s_half, 1)
            pool.memset(powers[:, Q:Q + 1], 0.0).then_inc(s_half, 1)
            pool.memset(comb_part[:, :, :, :], 0.0).then_inc(s_zeroed, 1)
            pool.memset(b2_f[:, :], 0.0).then_inc(s_zeroed, 1)
            pool.wait_ge(s_idx, 16)
            pick(0)
            pool.wait_ge(picked.sem, picked.at(0))
            gather(0)
            pool.wait_ge(s_half, 2)
            pool.wait_ge(s_cf, 16)
            for b in (0, 1):
                embed(b)
                pick(b + 1)
                pool.wait_ge(picked.sem, picked.at(b + 1))
                pool.wait_ge(embedded.sem, embedded.at(b))
                gather(b + 1)
                if b == 0:
                    norm1(0)

            def body(i):
                norm1(i + 1)
                if has(i + 2):
                    embed(i + 2)
                if has(i + 3):
                    pick(i + 3)
                    pool.wait_ge(picked.sem, picked.at(i + 3))
                    pool.wait_ge(embedded.sem, embedded.at(i + 2))
                norm2(i)
                if has(i + 3):
                    gather(i + 3)

            for i in (0, 1):
                body(i)
            with pool.Fori(2, B - 3) as i:
                body(i)
            for i in range(B - 3, B):
                body(i)

        @block.scalar
        def _(act):
            act.dma_start(wqkv[:, :], w_qkv).then_inc(s_attw, 16)
            act.dma_start(bcol[:, :], b_qkv).then_inc(s_attw, 16)
            act.dma_start(cb_f[:, :], const_b).then_inc(s_cbf, 16)
            act.wait_ge(s_cbf, 16)
            act.activation(cb[:, :], cb_f[:, :], ACT.Copy).then_inc(s_cb, 1)
            act.wait_ge(s_moew, 16 * 15)
            act.activation(w1_hi[:, :], w1_f[:, :], ACT.Copy).then_inc(s_w1hi, 1)

            def to_sbuf_1(b):
                act.wait_ge(xT_ps.sem, xT_ps.at(b))
                if has(b - 1):
                    act.wait_ge(scored.sem, scored.at(b - 1))
                    act.wait_ge(v_done.sem, v_done.at(b - 1))
                act.activation(xT[:, :], bT[:, :], ACT.Copy).then_inc(xT_sb.sem, 1)

            def to_sbuf_2(b):
                act.wait_ge(x2T_ps.sem, x2T_ps.at(b))
                if has(b - 1):
                    act.wait_ge(hidden.sem, hidden.at(b - 1))
                act.activation(x2T[:, :], bT[:, :], ACT.Copy).then_inc(x2T_sb.sem, 1)

            def exp_tile(b, q):
                n = (q + 1) * P
                act.wait_ge(shifted.sem, shifted.at(b, q + 1))
                if has(b - 1):
                    act.wait_ge(turned.sem, turned.at(b - 1, q + 1))
                    act.wait_ge(inverted.sem, inverted.at(b - 1))
                act.activation(probs[:, q, 0:n], bS[q % 2][:, 0:n], ACT.Exp, bias=shift[:, q:q + 1],
                               accum_out=row_sum[:, q:q + 1]).then_inc(exped.sem, 1)

            def move_turned(b, q):
                act.wait_ge(turned.sem, turned.at(b, q + 1))
                if has(b - 1):
                    act.wait_ge(attended.sem, attended.at(b - 1, q + 1))
                act.activation(pT[:, q, 0:q + 1, :], bX[:, 0:(q + 1) * P].rearrange("p (j t) -> p j t", t=P),
                               ACT.Copy).then_inc(pT_act.sem, 1)

            def gelu_pair(b, a):
                act.wait_ge(hidden.sem, hidden.at(b, a + 1))
                if a >= 2:
                    act.wait_ge(scaled.sem, scaled.at(b, a - 1))
                elif has(b - 1):
                    act.wait_ge(scaled.sem, scaled.at(b - 1, a + 3))
                act.activation(hg[:, a % 2, :], bS[a % 2][:, :], ACT.Gelu, bias=b1_col[:, a:a + 1])\
                    .then_inc(gelued.sem, 1)

            def keep_output(b):
                act.wait_ge(mixed.sem, mixed.at(b))
                if has(b - 1):
                    act.wait_ge(unmixed.sem, unmixed.at(b - 1))
                act.activation(yT[:, :], bY[0:D, :], ACT.Copy).then_inc(yT_sb.sem, 1)

            def body(i):
                if has(i):
                    act.wait_ge(g_ps.sem, g_ps.at(i))
                    if peeled(i, 0):
                        act.wait_ge(s_prep, PREP_C)
                    act.activation(g_hi[:, :], bG[:, :], ACT.Identity, bias=c_col[:, 0:1])\
                        .then_inc(g_hi_sb.sem, 1)
                if has(i - 1):
                    to_sbuf_2(i - 1)
                if has(i):
                    exp_tile(i, 0)
                    exp_tile(i, 1)
                if has(i - 1):
                    act.wait_ge(route.sem, route.at(i - 1, 2))
                    act.activation(top_e[:, :, :], top_d[:, :, :], ACT.Exp).then_inc(route_exp.sem, 1)
                if has(i):
                    exp_tile(i, 2)
                    move_turned(i, 1)
                    exp_tile(i, 3)
                if has(i - 2):
                    keep_output(i - 2)
                if has(i):
                    move_turned(i, 3)
                if has(i - 1):
                    for a in range(PAIRS):
                        gelu_pair(i - 1, a)
                if has(i + 1):
                    to_sbuf_1(i + 1)

            to_sbuf_1(0)
            pipeline(act, body)

        @block.tensor
        def _(pe):
            def turn_norm(k, b, done):
                pe.wait_ge(ln_pool[k].sem, ln_pool[k].at(b))
                if k == 0 and has(b - 2):
                    pe.wait_ge(x2T_sb.sem, x2T_sb.at(b - 2))
                elif k == 0 and has(b - 1):
                    pe.wait_ge(xT_sb.sem, xT_sb.at(b - 1))
                if k == 1 and has(b + 1):
                    pe.wait_ge(xT_sb.sem, xT_sb.at(b + 1))
                elif k == 1:
                    pe.wait_ge(x2T_sb.sem, x2T_sb.at(b - 1))
                for q in range(Q):
                    last = pe.transpose(bT[:, q * P:q * P + P],
                                        ln[k]["xs"][:, q, :, :].rearrange("p h d -> p (h d)"), ident)
                last.then_inc(done.sem, 1)

            def project_g(b):
                pe.wait_ge(xT_sb.sem, xT_sb.at(b))
                if has(b - 2):
                    pe.wait_ge(scaled.sem, scaled.at(b - 2, PAIRS))
                if has(b - 1):
                    pe.wait_ge(g_lo_sb.sem, g_lo_sb.at(b - 1))
                pe.matmul(bG[:, :], a_hi[:, :], xT[:, :], start=True, stop=False)
                pe.matmul(bG[:, :], a_lo[:, :], xT[:, :], start=False, stop=True).then_inc(g_ps.sem, 1)

            def project_v(b):
                if has(b - 2):
                    pe.wait_ge(ct_ready.sem, ct_ready.at(b - 2))
                for q in range(Q):
                    tile = xT[:, q * P:q * P + P]
                    pe.matmul(v_ps[:, q, :], tile, wv_hi[:, :], start=True, stop=False)
                    last = pe.matmul(v_ps[:, q, :], tile, wv_lo[:, :], start=False, stop=True)
                last.then_inc(v_done.sem, 1)

            def score_tile(b, q):
                n = (q + 1) * P
                if q == 0:
                    pe.wait_ge(g_lo_sb.sem, g_lo_sb.at(b))
                if q >= 2:
                    pe.wait_ge(exped.sem, exped.at(b, q - 1))
                elif has(b - 2):
                    pe.wait_ge(gelued.sem, gelued.at(b - 2, q + 3))
                elif has(b - 1):
                    pe.wait_ge(exped.sem, exped.at(b - 1, q + 3))
                tile = slice(q * P, q * P + P)
                pe.matmul(bS[q % 2][:, 0:n], g_hi[:, tile], xT[:, 0:n], start=True, stop=False)
                pe.matmul(bS[q % 2][:, 0:n], g_lo[:, tile], xT[:, 0:n], start=False, stop=False)
                pe.matmul(bS[q % 2][:, q * P:n], ident_b, mask, start=False, stop=True).then_inc(scored.sem, 1)

            def bX_free(b, q):
                if q >= 1:
                    before = pT_act if (q - 1) % 2 else pT_dve
                    pe.wait_ge(before.sem, before.at(b, (q - 1) // 2 + 1))
                elif has(b - 2):
                    pe.wait_ge(scaled.sem, scaled.at(b - 2, PAIRS - 1))
                elif has(b - 1):
                    pe.wait_ge(pT_act.sem, pT_act.at(b - 1))

            def turn_probs(b, q):
                pe.wait_ge(exped.sem, exped.at(b, q + 1))
                bX_free(b, q)
                for j in range(q + 1):
                    last = pe.transpose(bX[:, j * P:j * P + P], probs[:, q, j * P:j * P + P], ident)
                last.then_inc(turned.sem, 1)

            def attend(b, q):
                moved = pT_act if q % 2 else pT_dve
                pe.wait_ge(moved.sem, moved.at(b, q // 2 + 1))
                if q == 0:
                    pe.wait_ge(v_ready.sem, v_ready.at(b))
                    if has(b - 1):
                        pe.wait_ge(added.sem, added.at(b - 1))
                for j in range(q + 1):
                    last = pe.matmul(o_ps[:, q, :], pT[:, q, j, :], v_sb[:, j, 0:D], start=(j == 0), stop=(j == q))
                last.then_inc(attended.sem, 1)

            def logits(b):
                pe.wait_ge(x2T_sb.sem, x2T_sb.at(b))
                if has(b + 1):
                    pe.wait_ge(v_ready.sem, v_ready.at(b + 1))
                for q in range(Q):
                    tile = x2T[:, q * P:q * P + P]
                    pe.matmul(l_ps[:, q, :], tile, r_hi[:, :], start=True, stop=False)
                    last = pe.matmul(l_ps[:, q, :], tile, r_lo[:, :], start=False, stop=True)
                last.then_inc(routed_ps.sem, 1)

            def turn_weights(b):
                pe.wait_ge(route.sem, route.at(b))
                if has(b + 1):
                    pe.wait_ge(v_ready.sem, v_ready.at(b + 1))
                for q in range(Q):
                    last = pe.transpose(ct_ps[0:KB, q * P:q * P + P],
                                        comb_part[:, q, :, :].rearrange("p n k -> p (n k)"), ident_b)
                last.then_inc(ct_done.sem, 1)

            def first_layer(b, a):
                cols = slice(a * P, a * P + P)
                if a >= 2:
                    pe.wait_ge(gelued.sem, gelued.at(b, a - 1))
                elif has(b + 1):
                    pe.wait_ge(exped.sem, exped.at(b + 1, a + 3))
                pe.matmul(bS[a % 2][:, :], w1_hi[:, cols], x2T[:, :], start=True, stop=False)
                pe.matmul(bS[a % 2][:, :], w1_lo[:, cols], x2T[:, :], start=False, stop=True)\
                    .then_inc(hidden.sem, 1)
                if a == 0:
                    pe.wait_ge(ct_ready.sem, ct_ready.at(b))
                    if has(b + 1):
                        pe.wait_ge(pT_act.sem, pT_act.at(b + 1))
                if a == 1 and has(b + 1):
                    pe.wait_ge(g_lo_sb.sem, g_lo_sb.at(b + 1))
                if a >= 2:
                    pe.wait_ge(scaled.sem, scaled.at(b, a - 1))
                pe.matmul(w_bank[a % 2][:, :], select[0:KC, a, :], cT[0:KC, :], start=True, stop=True)\
                    .then_inc(spread.sem, 1)

            def second_layer(b, a):
                pe.wait_ge(scaled.sem, scaled.at(b, a + 1))
                if a == 0 and has(b - 1):
                    pe.wait_ge(finished.sem, finished.at(b - 1))
                pe.matmul(bY[0:D, :], w2_sb[:, a, :], hs[:, a, :], start=(a == 0), stop=False)
                if a == PAIRS - 1:
                    pe.matmul(bY[0:D, :], b2_rows[:, :], cT[:, :], start=False, stop=True).then_inc(mixed.sem, 1)

            def turn_output(b):
                constant_wait(pe)
                pe.wait_ge(yT_sb.sem, yT_sb.at(b))
                for q in range(Q):
                    last = pe.transpose(y_ps[:, q, :], yT[:, q * P:q * P + P], ident[0:D, 0:D])
                last.then_inc(unmixed.sem, 1)

            def set_up():
                pe.wait_ge(s_cf, 16)
                pe.wait_ge(s_attw, 32)
                for n in range(3):
                    last = pe.transpose(bM[0:D, n * D:n * D + D], wqkv[:, n * D:n * D + D], ident[0:D, 0:D])
                last.then_inc(s_wt_ps, 1)
                pe.wait_ge(s_wt, 1)
                pe.wait_ge(s_prep, PREP_BV)
                pe.wait_ge(s_wp, 32)
                twice = [wT[:, n, :, :].rearrange("d h i -> d (h i)") for n in range(3)]
                pe.matmul(bG[:, 0:P], twice[0], twice[1], start=True, stop=True)
                pe.matmul(bG[:, P:P + 1], twice[1], bcol[:, 0:1], start=True, stop=True)
                pe.matmul(bG[:, 2 * P:2 * P + D], twice[2], wp[:, :], start=True, stop=True)
                pe.matmul(bG[:, 2 * P + D:2 * P + D + 1], twice[0], bcol[:, 1:2], start=True, stop=True)
                pe.matmul(bG[:, 3 * P:3 * P + D], bv_rows[:, :], wp[:, :], start=True, stop=True)
                pe.matmul(bG[:, 3 * P + D:3 * P + D + 1], bq_rows[:, :], bcol[:, 1:2], start=True, stop=True)\
                    .then_inc(s_ab_ps, 1)

            def body(i):
                if has(i):
                    project_g(i)
                if has(i - 1):
                    turn_norm(1, i - 1, x2T_ps)
                if has(i):
                    if peeled(i, 0):
                        pe.wait_ge(s_prep, PREP_WVLO)
                    project_v(i)
                if has(i - 2):
                    second_layer(i - 2, 0)
                if has(i):
                    score_tile(i, 0)
                    score_tile(i, 1)
                if peeled(i, 1):
                    pe.wait_ge(s_prep, PREP_ALL)
                if has(i - 1):
                    logits(i - 1)
                if has(i - 2):
                    second_layer(i - 2, 1)
                if has(i):
                    turn_probs(i, 0)
                    score_tile(i, 2)
                if has(i - 2):
                    second_layer(i - 2, 2)
                if has(i):
                    turn_probs(i, 1)
                    score_tile(i, 3)
                    attend(i, 0)
                if has(i - 2):
                    second_layer(i - 2, 3)
                if has(i):
                    turn_probs(i, 2)
                    attend(i, 1)
                    turn_probs(i, 3)
                    attend(i, 2)
                    attend(i, 3)
                if has(i - 2):
                    turn_output(i - 2)
                if has(i - 1):
                    turn_weights(i - 1)
                    for a in range(PAIRS):
                        first_layer(i - 1, a)
                if has(i + 1):
                    turn_norm(0, i + 1, xT_ps)

            set_up()
            pe.wait_ge(s_prep, PREP_ALO)
            turn_norm(0, 0, xT_ps)
            pe.wait_ge(s_cb, 1)
            pipeline(pe, body)

        @block.vector
        def _(dve):
            def prep(ins, step):
                ins.then_inc(s_prep, 1)
                dve.wait_ge(s_prep, step)

            def statistics(k, b):
                n, mine = ln[k], ln_dve[k]
                for q in range(Q):
                    last = dve.bn_stats(n["stats"][:, q, :], stream[:, b, q, :])
                last.then_inc(mine.sem, 1)

            def aggregate(k, b):
                n, mine = ln[k], ln_dve[k]
                dve.wait_ge(mine.sem, mine.at(b, 1))
                dve.tensor_tensor(n["diff"][:, :], n["stats"][:, :, 1], n["stats"][:, :, 4], ALU.subtract)
                dve.tensor_tensor(n["both"][:, :, :], n["stats"][:, :, 1:3], n["stats"][:, :, 4:6], ALU.add)\
                    .then_inc(mine.sem, 1)
                dve.wait_ge(mine.sem, mine.at(b, 2))
                dve.scalar_tensor_tensor(out=n["between"][:, :], in0=n["diff"][:, :], scalar=0.25,
                                         in1=n["diff"][:, :], op0=ALU.mult, op1=ALU.mult)
                dve.tensor_scalar(n["within"][:, :], n["both"][:, :, 1], 1.0 / D, EPS, ALU.mult, ALU.add)
                dve.tensor_scalar(n["mean"][:, :], n["both"][:, :, 0], 0.5, None, ALU.mult).then_inc(mine.sem, 1)
                dve.wait_ge(mine.sem, mine.at(b, 3))
                if has(b - 1):
                    dve.wait_ge(ln_pool[k].sem, ln_pool[k].at(b - 1, 1))
                dve.tensor_tensor(n["var"][:, :], n["between"][:, :], n["within"][:, :], ALU.add)\
                    .then_inc(mine.sem, 1)

            def normalise(k, b):
                n, mine = ln[k], ln_dve[k]
                dve.wait_ge(ln_pool[k].sem, ln_pool[k].at(b, 1))
                if has(b - 1):
                    dve.wait_ge(ln_pool[k].sem, ln_pool[k].at(b - 1))
                    if k == 1:
                        dve.wait_ge(resid.sem, resid.at(b - 1))
                for q in range(Q):
                    last = dve.tensor_scalar(n["xn"][:, q, :], stream[:, b, q, :], n["mean"][:, q:q + 1],
                                             n["rstd"][:, q:q + 1], ALU.subtract, ALU.mult)
                last.then_inc(mine.sem, 1)

            def norm1_start(b):
                if has(b):
                    constant_wait(dve)
                    dve.wait_ge(embedded.sem, embedded.at(b))
                    statistics(0, b)
                    aggregate(0, b)

            def g_low(b):
                dve.wait_ge(g_hi_sb.sem, g_hi_sb.at(b))
                dve.scalar_tensor_tensor(out=g_lo[:, :], in0=bG[:, :], scalar=c_col[:, 0:1],
                                         in1=g_hi[:, :].bitcast(F32), op0=ALU.add, op1=ALU.subtract)\
                    .then_inc(g_lo_sb.sem, 1)

            def values(b):
                dve.wait_ge(v_done.sem, v_done.at(b))
                dve.tensor_tensor(v_sb[:, :, :], v_ps, v_bias[:, :].unsqueeze(1).to_broadcast([P, Q, VW]),
                                  ALU.add).then_inc(v_ready.sem, 1)

            def maximum(b, q):
                n = (q + 1) * P
                dve.wait_ge(scored.sem, scored.at(b, q + 1))
                dve.tensor_reduce(row_max[:, q:q + 1], bS[q % 2][:, 0:n], AXX, ALU.max, negate=True)\
                    .then_inc(maxed.sem, 1)
                dve.wait_ge(maxed.sem, maxed.at(b, q + 1))
                if q == 0:
                    dve.wait_ge(v_ready.sem, v_ready.at(b))
                    if has(b - 1):
                        dve.wait_ge(exped.sem, exped.at(b - 1))
                dve.tensor_scalar(shift[:, q:q + 1], row_max[:, q:q + 1], v_sb[:, q, D:D + 1], v_sb[:, q, D:D + 1],
                                  ALU.subtract, ALU.add).then_inc(shifted.sem, 1)

            def move_turned(b, q):
                dve.wait_ge(turned.sem, turned.at(b, q + 1))
                dve.tensor_copy(pT[:, q, 0:q + 1, :], bX[:, 0:(q + 1) * P].rearrange("p (j t) -> p j t", t=P))\
                    .then_inc(pT_dve.sem, 1)

            def add_attention(b):
                dve.wait_ge(exped.sem, exped.at(b))
                dve.reciprocal(row_inv[:, :], row_sum[:, :]).then_inc(inverted.sem, 1)
                dve.wait_ge(inverted.sem, inverted.at(b))
                dve.wait_ge(attended.sem, attended.at(b))
                for q in range(Q):
                    last = dve.scalar_tensor_tensor(out=stream[:, b, q, :], in0=o_ps[:, q, :],
                                                    scalar=row_inv[:, q:q + 1], in1=stream[:, b, q, :],
                                                    op0=ALU.mult, op1=ALU.add)
                last.then_inc(added.sem, 1)

            def route_steps(b):
                def done(ins, step):
                    ins.then_inc(route.sem, 1)

                def after(step):
                    dve.wait_ge(route.sem, route.at(b, step))

                def comb_parts(n):
                    return comb_part[:, :, :, n * E:n * E + E]

                rest = comb_rest[:, :, :].unsqueeze(2).to_broadcast([P, Q, SPLIT, E])

                constant_wait(dve)
                dve.wait_ge(routed_ps.sem, routed_ps.at(b))
                for q in range(Q):
                    last = dve.max(top[:, q, :], l_ps[:, q, :])
                done(last, 1)
                yield
                after(1)
                if has(b - 1):
                    dve.wait_ge(route_exp.sem, route_exp.at(b - 1))
                done(dve.tensor_tensor(top_d[:, :, :], top[:, :, :], top[:, :, 0:1].to_broadcast([P, Q, E]),
                                       ALU.subtract), 2)
                for q in range(Q):
                    last = dve.max_index(top_i[:, q, :], top[:, q, :], l_ps[:, q, :])
                done(last, 3)
                yield
                after(3)
                done(dve.tensor_tensor(chosen[:, :, :, :],
                                       top_i[:, :, 0:TOPK].unsqueeze(3).to_broadcast([P, Q, TOPK, E]),
                                       iota.unsqueeze(1).unsqueeze(1).to_broadcast([P, Q, TOPK, E]),
                                       ALU.is_equal), 4)
                yield
                dve.wait_ge(route_exp.sem, route_exp.at(b))
                done(dve.tensor_reduce(esum[:, :, 0], top_e[:, :, :], AXX, ALU.add), 5)
                done(dve.tensor_tensor(pair_sum[:, :, :], top_e[:, :, 0:1], top_e[:, :, 1:2], ALU.add), 6)
                yield
                after(6)
                done(dve.scalar_tensor_tensor(out=denom[:, :, 0], in0=esum[:, :, 0], scalar=GUARD,
                                              in1=pair_sum[:, :, 0], op0=ALU.mult, op1=ALU.max), 7)
                yield
                after(7)
                done(dve.reciprocal(inv[:, :, :], denom[:, :, :]), 8)
                yield
                after(8)
                done(dve.tensor_tensor(weight[:, :, :], top_e[:, :, 0:TOPK],
                                       inv[:, :, :].to_broadcast([P, Q, TOPK]), ALU.mult), 9)
                yield
                after(9)
                done(dve.tensor_tensor(placed[:, :, :, :], chosen[:, :, :, :],
                                       weight[:, :, :].unsqueeze(3).to_broadcast([P, Q, TOPK, E]), ALU.mult), 10)
                yield
                after(10)
                done(dve.tensor_tensor(comb[:, :, :], placed[:, :, 0, :], placed[:, :, 1, :], ALU.add), 11)
                yield
                after(11)
                if has(b - 1):
                    dve.wait_ge(ct_done.sem, ct_done.at(b - 1))
                done(dve.tensor_copy(comb_parts(0), comb[:, :, :].unsqueeze(2).to_broadcast([P, Q, SPLIT, E])), 12)
                yield
                after(12)
                done(dve.tensor_tensor(comb_rest[:, :, :], comb[:, :, :], comb_part[:, :, 0, 0:E],
                                       ALU.subtract), 13)
                yield
                after(13)
                done(dve.tensor_copy(comb_parts(1), rest), 14)
                yield
                after(14)
                done(dve.tensor_tensor(comb_parts(2), rest, comb_parts(1), ALU.subtract), 15)

            def keep_weights(b):
                dve.wait_ge(ct_done.sem, ct_done.at(b))
                if has(b - 1):
                    dve.wait_ge(mixed.sem, mixed.at(b - 1))
                dve.tensor_copy(cT[:, :], ct_ps[0:KB, :]).then_inc(ct_ready.sem, 1)

            def scale_pair(b, a):
                dve.wait_ge(gelued.sem, gelued.at(b, a + 1))
                dve.wait_ge(spread.sem, spread.at(b, a + 1))
                dve.tensor_tensor(hs[:, a, :], w_bank[a % 2][:, :], hg[:, a % 2, :], ALU.mult)\
                    .then_inc(scaled.sem, 1)

            def finish(b):
                dve.wait_ge(unmixed.sem, unmixed.at(b))
                dve.wait_ge(resid.sem, resid.at(b))
                dve.tensor_tensor(stream[:, b], y_ps, stream[:, b], ALU.add).then_inc(finished.sem, 1)

            def split_weights(hi, lo, full, step):
                prep(dve.tensor_copy(hi, full), step)
                prep(dve.tensor_tensor(lo, full, hi.bitcast(F32), ALU.subtract), step + 1)

            def set_up_attention():
                dve.wait_ge(s_attw, 32)
                prep(dve.tensor_copy(bq_rows[:, :], bcol[:, 0:1].to_broadcast([D, P])), PREP_BQ)
                prep(dve.tensor_copy(bv_rows[:, :], bcol[:, 2:3].to_broadcast([D, P])), PREP_BV)
                dve.wait_ge(s_wt_ps, 1)
                dve.tensor_copy(wT[:, :, :, :], bM[0:D, 0:3 * D].rearrange("d (t i) -> d t i", t=3).unsqueeze(2)
                                .to_broadcast([D, 3, 2, D])).then_inc(s_wt, 1)
                dve.wait_ge(s_ab_ps, 1)
                prep(dve.tensor_scalar(c_col[:, :], bG[:, P:P + 1], SCALE, None, ALU.mult), PREP_C)
                prep(dve.tensor_scalar(a_hi[:, :], bG[:, 0:P], SCALE, None, ALU.mult), PREP_AHI)
                prep(dve.scalar_tensor_tensor(out=a_lo[:, :], in0=bG[:, 0:P], scalar=SCALE,
                                              in1=a_hi[:, :].bitcast(F32), op0=ALU.mult, op1=ALU.subtract), PREP_ALO)
                wv, vb = bG[:, 2 * P:2 * P + D + 1], bG[:, 3 * P:3 * P + D + 1]
                prep(dve.tensor_copy(wv_f[:, 0:D], wv[:, 0:D]), PREP_WV)
                prep(dve.tensor_scalar(wv_f[:, D:D + 1], wv[:, D:D + 1], SCALE, None, ALU.mult), PREP_WU)
                prep(dve.memset(wv_f[:, D + 1:VW], 0.0), PREP_WPAD)
                dve.wait_ge(s_wp, 32)
                prep(dve.tensor_tensor(v_bias[:, 0:D], vb[:, 0:D], bp[:, :], ALU.add), PREP_VB)
                prep(dve.tensor_scalar(v_bias[:, D:D + 1], vb[:, D:D + 1], SCALE, None, ALU.mult), PREP_VK)
                prep(dve.memset(v_bias[:, D + 1:VW], 0.0), PREP_VPAD)
                split_weights(wv_hi[:, :], wv_lo[:, :], wv_f[:, :], PREP_WVHI)

            def set_up_experts():
                dve.wait_ge(s_moew, 16 * 15)
                split_weights(r_hi[:, :], r_lo[:, :], r_f[:, :], PREP_RHI)
                dve.wait_ge(s_w1hi, 1)
                prep(dve.tensor_tensor(w1_lo[:, :], w1_f[:, :], w1_hi[:, :].bitcast(F32), ALU.subtract), PREP_W1LO)
                for n in range(SPLIT):
                    left = b2_f[:, :] if n == 0 else b2_rest[:, n - 1, :]
                    prep(dve.tensor_copy(b2_part[:, n, :], left), PREP_B2 + 3 * n)
                    if n < SPLIT - 1:
                        prep(dve.tensor_tensor(b2_rest[:, n, :], left, b2_part[:, n, :], ALU.subtract),
                             PREP_B2 + 3 * n + 1)
                    rows_n = slice(n * KG, n * KG + KG)
                    prep(dve.tensor_copy(b2_rows[rows_n, :], b2_part[rows_n, n, :]),
                         PREP_B2 + 3 * n + (2 if n < SPLIT - 1 else 1))

            def body(i):
                def routing():
                    next(pending, None)

                pending = route_steps(i - 1) if has(i - 1) else iter(())
                if has(i):
                    g_low(i)
                    values(i)
                    maximum(i, 0)
                    maximum(i, 1)
                norm1_start(i + 1)
                routing()
                routing()
                routing()
                if has(i):
                    move_turned(i, 0)
                    maximum(i, 2)
                routing()
                if has(i + 1):
                    normalise(0, i + 1)
                routing()
                if has(i):
                    maximum(i, 3)
                routing()
                routing()
                if has(i):
                    move_turned(i, 2)
                for _ in range(9):
                    routing()
                if has(i - 1):
                    keep_weights(i - 1)
                if has(i - 2):
                    finish(i - 2)
                if has(i):
                    add_attention(i)
                    constant_wait(dve)
                    dve.wait_ge(added.sem, added.at(i))
                    statistics(1, i)
                if has(i - 1):
                    scale_pair(i - 1, 0)
                if has(i):
                    aggregate(1, i)
                if has(i - 1):
                    scale_pair(i - 1, 1)
                if has(i):
                    normalise(1, i)
                if has(i - 1):
                    scale_pair(i - 1, 2)
                    scale_pair(i - 1, 3)

            set_up_attention()
            dve.wait_ge(s_zeroed, 2)
            norm1_start(0)
            normalise(0, 0)
            set_up_experts()
            pipeline(dve, body)


def constants():
    f = np.zeros((P, C_F32), np.float32)
    f[:, C_ID:C_ID + P] = np.eye(P)
    d = np.arange(D)
    exponent = (d - d % 2).astype(np.float32) / np.float32(D)
    inv_freq = np.power(np.float32(10000.0), -exponent)
    angle = np.arange(T, dtype=np.float32)[:, None] * inv_freq
    table = np.where(d % 2 == 0, np.sin(angle), np.cos(angle)).astype(np.float32)
    f[:, C_PE:C_PE + Q * D] = table.reshape(Q, P, D).transpose(1, 0, 2).reshape(P, Q * D)
    f[:, C_IOTA:C_IOTA + E] = np.arange(E)
    b = np.zeros((P, C_BF16), np.float32)
    b[:, C_ID:C_ID + P] = np.eye(P)
    b[:, C_MASK:C_MASK + P] = np.where(np.arange(P)[None, :] > np.arange(P)[:, None], MASKED, 0.0)
    for a in range(PAIRS):
        for part in range(SPLIT):
            for e in range(2):
                at = C_SEL + a * P + e * D
                b[part * E + 2 * a + e, at:at + D] = 1.0
    return f, b


def kernel(x, L0_tok_W, L0_attn_W_qkv, L0_attn_b_qkv, L0_attn_W_proj, L0_attn_b_proj, L0_ffn_router_w,
           L0_ffn_w1, L0_ffn_b1, L0_ffn_w2, L0_ffn_b2):
    import concourse.bacc as bacc
    from concourse.bass_utils import run_bass_kernel_spmd as run

    f, b = constants()
    arrays = {
        "ids": np.ascontiguousarray(np.asarray(x).reshape(B * Q, P).T),
        "table": L0_tok_W, "w_qkv": L0_attn_W_qkv, "b_qkv": np.asarray(L0_attn_b_qkv).reshape(3, D).T, "w_proj": L0_attn_W_proj,
        "b_proj": L0_attn_b_proj, "router": np.asarray(L0_ffn_router_w).T, "w1": L0_ffn_w1, "b1": np.asarray(L0_ffn_b1).reshape(PAIRS, P).T,
        "w2": L0_ffn_w2, "b2": L0_ffn_b2, "const": f, "const_b": b,
    }
    arrays = {name: np.ascontiguousarray(a) for name, a in arrays.items()}
    nc = bacc.Bacc("TRN2", target_bir_lowering=False, num_devices=1)
    aps = {name: nc.dram_tensor(name, a.shape, mybir.dt.from_np(a.dtype), kind="ExternalInput").ap()
           for name, a in arrays.items()}
    out = nc.dram_tensor("out", (B, T, D), F32, kind="ExternalOutput").ap()
    build(nc, **aps, out=out)
    return run(nc, [arrays], core_ids=[0]).results[0]["out"]
```

```python
from contextlib import ExitStack

import numpy as np
import concourse.bass as bass
from concourse import mybir

F32 = mybir.dt.float32
F32R = mybir.dt.float32r
BF16 = mybir.dt.bfloat16
U32 = mybir.dt.uint32
I32 = mybir.dt.int32
ALU = mybir.AluOpType
ACT = mybir.ActivationFunctionType
AXX = mybir.AxisListType.X

B, T, D = 8, 512, 64
E, TOPK = 8, 2
P = 128
Q = T // P
PAIRS = E * D // P
VW = D + 2
SPLIT = 3
KC = SPLIT * E
KG = 32
KB = SPLIT * KG
EPS = 1e-5
SCALE = float(D) ** -0.5
GUARD = 1e-12
MASKED = -1e30

C_ID, C_PE, C_IOTA, C_F32 = 0, P, P + Q * D, P + Q * D + E
C_MASK, C_SEL, C_BF16 = P, 2 * P, 2 * P + PAIRS * P


class Steps:

    def __init__(self, sem, per=1):
        self.sem, self.per = sem, per

    def at(self, batch, step=None):
        return batch * self.per + (self.per if step is None else step)


def build(nc, ids, table, w_qkv, b_qkv, w_proj, b_proj, router, w1, b1, w2, b2, const, const_b, out):
    ctx = ExitStack()
    with ctx:
        def sb(name, shape, dt=F32):
            return ctx.enter_context(nc.sbuf_tensor(name, shape, dt))

        def bank(name):
            return ctx.enter_context(nc.psum_tensor(name, [P, 512], F32))

        def sem(name):
            return ctx.enter_context(nc.semaphore(name))

        def steps(name, per=1):
            return Steps(sem(name), per)

        cf = sb("cf", [P, C_F32])
        cb_f = sb("cb_f", [P, C_BF16])
        cb = sb("cb", [P, C_BF16], BF16)
        ident = cf[:, C_ID:C_ID + P]
        pos = cf[:, C_PE:C_PE + Q * D].rearrange("p (q d) -> p q d", q=Q)
        iota = cf[:, C_IOTA:C_IOTA + E]
        ident_b = cb[:, C_ID:C_ID + P]
        mask = cb[:, C_MASK:C_MASK + P]
        select = cb[:, C_SEL:C_SEL + PAIRS * P].rearrange("k (a m) -> k a m", a=PAIRS)
        idx = sb("idx", [P, B * Q], I32)
        idx_v = idx[:, :].rearrange("p (b q) -> p b q", q=Q)
        ids_now = sb("ids_now", [P, Q], I32)
        rows = sb("rows", [P, Q, D])
        wqkv = sb("wqkv", [D, 3 * D])
        bcol = sb("bcol", [D, 3])
        wp = sb("wp", [D, D])
        bp = sb("bp", [P, D])
        wT = sb("wT", [D, 3, 2, D])
        bq_rows = sb("bq_rows", [D, P])
        bv_rows = sb("bv_rows", [D, P])
        a_hi, a_lo = sb("a_hi", [P, P], F32R), sb("a_lo", [P, P], F32R)
        c_col = sb("c_col", [P, 1])
        wv_f = sb("wv_f", [P, VW])
        wv_hi, wv_lo = sb("wv_hi", [P, VW], F32R), sb("wv_lo", [P, VW], F32R)
        v_bias = sb("v_bias", [P, VW])
        r_f = sb("r_f", [P, E])
        r_hi, r_lo = sb("r_hi", [P, E], F32R), sb("r_lo", [P, E], F32R)
        w1_f = sb("w1_f", [P, E * D])
        w1_hi, w1_lo = sb("w1_hi", [P, E * D], F32R), sb("w1_lo", [P, E * D], F32R)
        b1_col = sb("b1_col", [P, PAIRS])
        w2_sb = sb("w2_sb", [P, PAIRS, D])
        b2_f = sb("b2_f", [KB, D])
        b2_rest = sb("b2_rest", [KB, 2, D])
        b2_part = sb("b2_part", [KB, SPLIT, D], BF16)
        b2_rows = sb("b2_rows", [KB, D], BF16)
        powers = sb("powers", [P, Q + 1])
        warm = sb("warm", [P, 1])

        stream = sb("stream", [P, B, Q, D])
        ln = []
        for k in (1, 2):
            ln.append(dict(
                stats=sb(f"stats{k}", [P, Q, 6]), diff=sb(f"diff{k}", [P, Q]), both=sb(f"both{k}", [P, Q, 2]),
                between=sb(f"between{k}", [P, Q]), within=sb(f"within{k}", [P, Q]), mean=sb(f"mean{k}", [P, Q]),
                var=sb(f"var{k}", [P, Q]), rstd=sb(f"rstd{k}", [P, Q]), xn=sb(f"xn{k}", [P, Q, D]), xs=sb(f"xs{k}", [P, Q, 2, D])))
        xT = sb("xT", [P, T], F32R)
        x2T = sb("x2T", [P, T], F32R)
        g_hi, g_lo = sb("g_hi", [P, T], F32R), sb("g_lo", [P, T], F32R)
        v_sb = sb("v_sb", [P, Q, VW])
        row_max = sb("row_max", [P, Q])
        shift = sb("shift", [P, Q])
        probs = sb("probs", [P, Q, T])
        row_sum = sb("row_sum", [P, Q])
        row_inv = sb("row_inv", [P, Q])
        pT = sb("pT", [P, Q, Q, P])
        top = sb("top", [P, Q, E])
        top_i = sb("top_i", [P, Q, E], U32)
        top_d = sb("top_d", [P, Q, E])
        top_e = sb("top_e", [P, Q, E])
        chosen = sb("chosen", [P, Q, TOPK, E])
        esum = sb("esum", [P, Q, 1])
        pair_sum = sb("pair_sum", [P, Q, 1])
        denom = sb("denom", [P, Q, 1])
        inv = sb("inv", [P, Q, 1])
        weight = sb("weight", [P, Q, TOPK])
        placed = sb("placed", [P, Q, TOPK, E])
        comb = sb("comb", [P, Q, E])
        comb_rest = sb("comb_rest", [P, Q, E])
        comb_part = sb("comb_part", [P, Q, SPLIT, KG], BF16)
        cT = sb("cT", [KB, T], BF16)
        hg = sb("hg", [P, PAIRS, T])
        hs = sb("hs", [P, PAIRS, T])
        yT = sb("yT", [D, T])

        bT = bank("bT")
        bG = bank("bG")
        bM = bank("bM")
        bS = [bank("bS0"), bank("bS1")]
        bX = bank("bX")
        bO = bank("bO")
        bY = bank("bY")
        v_ps = bM[:, 0:Q * VW].rearrange("p (q n) -> p q n", q=Q)
        l_ps = bM[:, Q * VW:Q * VW + Q * E].rearrange("p (q e) -> p q e", q=Q)
        ct_ps = bM[:, 0:T // 2].bitcast(BF16)
        o_ps = bO[:, 0:Q * D].rearrange("p (q d) -> p q d", q=Q)
        y_ps = bY[:, 0:Q * D].rearrange("p (q d) -> p q d", q=Q)
        w_bank = [bX, bT, bO, bG]

        s_idx, s_cf, s_cbf, s_cb = sem("s_idx"), sem("s_cf"), sem("s_cbf"), sem("s_cb")
        s_attw, s_wp, s_moew = sem("s_attw"), sem("s_wp"), sem("s_moew")
        s_half = sem("s_half")
        s_zeroed = sem("s_zeroed")
        s_wt_ps, s_wt, s_ab_ps = sem("s_wt_ps"), sem("s_wt"), sem("s_ab_ps")
        s_prep = sem("s_prep")
        s_w1hi = sem("s_w1hi")
        picked = steps("picked")
        gathered = steps("gathered", 16 * Q)
        embedded = steps("embedded")
        ln_dve = [steps("ln1_dve", 5), steps("ln2_dve", 5)]
        ln_pool = [steps("ln1_pool", 3), steps("ln2_pool", 3)]
        resid = steps("resid")
        xT_ps, xT_sb = steps("xT_ps"), steps("xT_sb")
        x2T_ps, x2T_sb = steps("x2T_ps"), steps("x2T_sb")
        g_ps, g_hi_sb, g_lo_sb = steps("g_ps"), steps("g_hi_sb"), steps("g_lo_sb")
        v_done, v_ready = steps("v_done"), steps("v_ready")
        scored = steps("scored", Q)
        maxed = steps("maxed", Q)
        shifted = steps("shifted", Q)
        exped = steps("exped", Q)
        turned = steps("turned", Q)
        moved = steps("moved", Q)
        attended = steps("attended", Q)
        inverted = steps("inverted")
        added = steps("added")
        routed_ps = steps("routed_ps")
        route = steps("route", 15)
        route_exp = steps("route_exp")
        ct_done, ct_ready = steps("ct_done"), steps("ct_ready")
        hidden = steps("hidden", PAIRS)
        spread = steps("spread", PAIRS)
        gelued = steps("gelued", PAIRS)
        scaled = steps("scaled", PAIRS)
        biased = steps("biased")
        mixed = steps("mixed", PAIRS)
        yT_sb = steps("yT_sb")
        unmixed = steps("unmixed")
        finished = steps("finished")
        s_store = sem("s_store")

        (PREP_BQ, PREP_BV, PREP_C, PREP_AHI, PREP_ALO, PREP_WV, PREP_WU, PREP_WPAD, PREP_VB, PREP_VK, PREP_VPAD,
         PREP_WVHI, PREP_WVLO, PREP_RHI, PREP_RLO, PREP_W1LO, PREP_B2) = range(1, 18)
        PREP_ALL = PREP_B2 + 3 * SPLIT - 2

        def has(batch):
            return not isinstance(batch, int) or 0 <= batch < B

        def peeled(i, n):
            return isinstance(i, int) and i == n

        def constant_wait(eng):
            eng.wait_ge(s_idx, 16)

        def pipeline(eng, body):
            for i in (0, 1, 2):
                body(i)
            with eng.Fori(3, B - 1) as i:
                body(i)
            for i in (B - 1, B, B + 1):
                body(i)

        block = ctx.enter_context(nc.Block())

        @block.sync
        def _(sp):
            sp.dma_start(idx[:, :], ids).then_inc(s_idx, 16)
            sp.dma_start(cf[:, :], const).then_inc(s_cf, 16)
            sp.dma_start(wp[:, :], w_proj).then_inc(s_wp, 16)
            sp.dma_start(bp[:, :], b_proj.partition_broadcast(P)).then_inc(s_wp, 16)
            for half in range(2):
                rows = slice(half * D, half * D + D)
                sp.dma_start(w1_f[rows, :].rearrange("i (e f) -> i e f", e=E),
                             w1.rearrange("e i f -> i e f")).then_inc(s_moew, 16)
                sp.dma_start(r_f[rows, :], router).then_inc(s_moew, 16)
            sp.dma_start(w2_sb[:, :, :], w2.rearrange("(a e) f d -> (e f) a d", e=2)).then_inc(s_moew, 16)
            sp.dma_start(b1_col[:, :], b1).then_inc(s_moew, 16)
            sp.wait_ge(s_zeroed, 2)
            for part in range(SPLIT):
                for copy in range(SPLIT):
                    at = copy * KG + part * E
                    sp.dma_start(b2_f[at:at + E, :], b2).then_inc(s_moew, 16)

            out_v = out.rearrange("b (q p) d -> b p q d", q=Q)
            with sp.Fori(0, B) as b:
                sp.wait_ge(finished.sem, finished.at(b))
                sp.dma_start(out_v[b], stream[:, b]).then_inc(s_store, 16)
            sp.wait_ge(s_store, 16 * B)

        @block.gpsimd
        def _(pool):
            def pick(b):
                pool.tensor_copy(ids_now[:, :], idx_v[:, b, :]).then_inc(picked.sem, 1)

            def gather(b):
                for q in range(Q):
                    pool.indirect_dma_start(
                        out=rows[:, q, :], out_offset=None, in_=table,
                        in_offset=bass.IndirectOffsetOnAxis(ap=ids_now[:, q:q + 1], axis=0),
                        bounds_check=table.shape[0] - 1).then_inc(gathered.sem, 16)

            def embed(b):
                pool.wait_ge(gathered.sem, gathered.at(b))
                pool.tensor_tensor(stream[:, b], rows[:, :, :], pos, ALU.add).then_inc(embedded.sem, 1)

            def may_gather(b):
                pool.wait_ge(picked.sem, picked.at(b))
                pool.wait_ge(embedded.sem, embedded.at(b - 1))

            def inverse_deviation(k, b):
                n, mine, dve = ln[k], ln_pool[k], ln_dve[k]
                pool.wait_ge(dve.sem, dve.at(b, 4))
                pool.tensor_tensor(n["rstd"][:, :], n["var"][:, :], powers[:, 0:Q], ALU.pow).then_inc(mine.sem, 1)

            def split(k, b, read):
                n, mine, dve = ln[k], ln_pool[k], ln_dve[k]
                pool.wait_ge(dve.sem, dve.at(b, 5))
                if has(b - 1):
                    pool.wait_ge(read.sem, read.at(b - 1))
                pool.tensor_tensor(n["xs"][:, :, 0, :].bitcast(F32R), n["xn"][:, :, :],
                                   powers[:, Q:Q + 1].unsqueeze(2).to_broadcast([P, Q, D]), ALU.add)\
                    .then_inc(mine.sem, 1)
                pool.wait_ge(mine.sem, mine.at(b, 2))
                pool.tensor_tensor(n["xs"][:, :, 1, :], n["xn"][:, :, :], n["xs"][:, :, 0, :], ALU.subtract)\
                    .then_inc(mine.sem, 1)

            def norm2(b):
                if has(b):
                    inverse_deviation(1, b)
                    split(1, b, x2T_ps)
                    pool.tensor_tensor(stream[:, b], stream[:, b], ln[1]["xn"][:, :, :], ALU.add)\
                        .then_inc(resid.sem, 1)

            pool.memset(powers[:, 0:Q], -0.5).then_inc(s_half, 1)
            pool.memset(powers[:, Q:Q + 1], 0.0).then_inc(s_half, 1)
            pool.memset(comb_part[:, :, :, :], 0.0).then_inc(s_zeroed, 1)
            pool.memset(b2_f[:, :], 0.0).then_inc(s_zeroed, 1)
            pool.wait_ge(s_idx, 16)
            pick(0)
            pool.wait_ge(picked.sem, picked.at(0))
            gather(0)
            pool.wait_ge(s_half, 2)
            pool.wait_ge(s_cf, 16)
            embed(0)

            def body(i):
                if has(i + 2):
                    pick(i + 2)
                if has(i + 1):
                    inverse_deviation(0, i + 1)
                if has(i + 2):
                    may_gather(i + 2)
                if has(i + 1):
                    split(0, i + 1, xT_ps)
                if has(i + 2):
                    gather(i + 2)
                    embed(i + 2)
                norm2(i)

            for i in (-1, 0, 1):
                body(i)
            with pool.Fori(2, B - 2) as i:
                body(i)
            for i in (B - 2, B - 1):
                body(i)

        @block.scalar
        def _(act):
            act.dma_start(wqkv[:, :], w_qkv).then_inc(s_attw, 16)
            act.dma_start(bcol[:, :], b_qkv).then_inc(s_attw, 16)
            act.dma_start(cb_f[:, :], const_b).then_inc(s_cbf, 16)
            act.wait_ge(s_cbf, 16)
            act.activation(cb[:, :], cb_f[:, :], ACT.Copy).then_inc(s_cb, 1)
            act.wait_ge(s_moew, 16 * 15)
            act.activation(w1_hi[:, :], w1_f[:, :], ACT.Copy).then_inc(s_w1hi, 1)

            def to_sbuf_1(b):
                act.wait_ge(xT_ps.sem, xT_ps.at(b))
                if has(b - 1):
                    act.wait_ge(scored.sem, scored.at(b - 1))
                    act.wait_ge(v_done.sem, v_done.at(b - 1))
                act.activation(xT[:, :], bT[:, :], ACT.Copy).then_inc(xT_sb.sem, 1)

            def to_sbuf_2(b):
                act.wait_ge(x2T_ps.sem, x2T_ps.at(b))
                if has(b - 1):
                    act.wait_ge(hidden.sem, hidden.at(b - 1))
                act.activation(x2T[:, :], bT[:, :], ACT.Copy).then_inc(x2T_sb.sem, 1)

            def exp_tile(b, q):
                n = (q + 1) * P
                act.wait_ge(shifted.sem, shifted.at(b, q + 1))
                if has(b - 1):
                    act.wait_ge(turned.sem, turned.at(b - 1, q + 1))
                    act.wait_ge(inverted.sem, inverted.at(b - 1))
                act.activation(probs[:, q, 0:n], bS[q % 2][:, 0:n], ACT.Exp, bias=shift[:, q:q + 1],
                               accum_out=row_sum[:, q:q + 1]).then_inc(exped.sem, 1)

            def move_turned(b, q):
                act.wait_ge(turned.sem, turned.at(b, q + 1))
                if has(b - 1):
                    act.wait_ge(attended.sem, attended.at(b - 1, q + 1))
                act.activation(pT[:, q, 0:q + 1, :], bX[:, 0:(q + 1) * P].rearrange("p (j t) -> p j t", t=P),
                               ACT.Copy).then_inc(moved.sem, 1)

            def gelu_pair(b, a):
                act.wait_ge(hidden.sem, hidden.at(b, a + 1))
                if has(b - 1):
                    act.wait_ge(scaled.sem, scaled.at(b - 1, a + 1))
                act.activation(hg[:, a, :], bS[a % 2][:, :], ACT.Gelu, bias=b1_col[:, a:a + 1])\
                    .then_inc(gelued.sem, 1)

            def keep_output(b):
                act.wait_ge(mixed.sem, mixed.at(b))
                if has(b - 1):
                    act.wait_ge(unmixed.sem, unmixed.at(b - 1))
                act.activation(yT[:, :], bY[0:D, :], ACT.Copy).then_inc(yT_sb.sem, 1)

            def load_function(func):
                act.activation(warm[:, :], powers[:, Q:Q + 1], func)

            def g_high(b):
                act.wait_ge(g_ps.sem, g_ps.at(b))
                act.activation(g_hi[:, :], bG[:, :], ACT.Identity, bias=c_col[:, 0:1]).then_inc(g_hi_sb.sem, 1)

            def body(i):
                if has(i):
                    exp_tile(i, 0)
                    exp_tile(i, 1)
                    move_turned(i, 0)
                if has(i - 1):
                    to_sbuf_2(i - 1)
                if has(i):
                    exp_tile(i, 2)
                    move_turned(i, 1)
                    exp_tile(i, 3)
                    move_turned(i, 2)
                if has(i - 1):
                    act.wait_ge(route.sem, route.at(i - 1, 2))
                    act.activation(top_e[:, :, :], top_d[:, :, :], ACT.Exp).then_inc(route_exp.sem, 1)
                if has(i):
                    move_turned(i, 3)
                if has(i - 1):
                    load_function(ACT.Gelu)
                if has(i + 1):
                    to_sbuf_1(i + 1)
                if has(i - 1):
                    gelu_pair(i - 1, 0)
                if has(i + 1):
                    g_high(i + 1)
                if has(i - 1):
                    gelu_pair(i - 1, 1)
                    gelu_pair(i - 1, 2)
                if has(i - 2):
                    keep_output(i - 2)
                if has(i - 1):
                    gelu_pair(i - 1, 3)
                if has(i) and not peeled(i, 0):
                    load_function(ACT.Exp)

            act.wait_ge(s_half, 2)
            to_sbuf_1(0)
            act.wait_ge(s_prep, PREP_C)
            g_high(0)
            pipeline(act, body)

        @block.tensor
        def _(pe):
            def turn_norm(k, b, done):
                pe.wait_ge(ln_pool[k].sem, ln_pool[k].at(b))
                if k == 0 and has(b - 2):
                    pe.wait_ge(x2T_sb.sem, x2T_sb.at(b - 2))
                elif k == 0 and has(b - 1):
                    pe.wait_ge(xT_sb.sem, xT_sb.at(b - 1))
                elif k == 1 and has(b - 1):
                    pe.wait_ge(scaled.sem, scaled.at(b - 1, 2))
                elif k == 1:
                    pe.wait_ge(xT_sb.sem, xT_sb.at(b + 1))
                for q in range(Q):
                    last = pe.transpose(bT[:, q * P:q * P + P],
                                        ln[k]["xs"][:, q, :, :].rearrange("p h d -> p (h d)"), ident)
                last.then_inc(done.sem, 1)

            def project_g(b):
                if has(b - 3):
                    pe.wait_ge(scaled.sem, scaled.at(b - 3))
                pe.wait_ge(xT_sb.sem, xT_sb.at(b))
                if has(b - 1):
                    pe.wait_ge(g_lo_sb.sem, g_lo_sb.at(b - 1))
                pe.matmul(bG[:, :], a_hi[:, :], xT[:, :], start=True, stop=False)
                pe.matmul(bG[:, :], a_lo[:, :], xT[:, :], start=False, stop=True).then_inc(g_ps.sem, 1)

            def project_v(b):
                if has(b - 2):
                    pe.wait_ge(ct_ready.sem, ct_ready.at(b - 2))
                for q in range(Q):
                    tile = xT[:, q * P:q * P + P]
                    pe.matmul(v_ps[:, q, :], tile, wv_hi[:, :], start=True, stop=False)
                    last = pe.matmul(v_ps[:, q, :], tile, wv_lo[:, :], start=False, stop=True)
                last.then_inc(v_done.sem, 1)

            def score_tile(b, q):
                n = (q + 1) * P
                if q == 0:
                    pe.wait_ge(g_lo_sb.sem, g_lo_sb.at(b))
                if q >= 2:
                    pe.wait_ge(exped.sem, exped.at(b, q - 1))
                elif has(b - 2):
                    pe.wait_ge(gelued.sem, gelued.at(b - 2, q + 3))
                elif has(b - 1):
                    pe.wait_ge(exped.sem, exped.at(b - 1, q + 3))
                tile = slice(q * P, q * P + P)
                pe.matmul(bS[q % 2][:, 0:n], g_hi[:, tile], xT[:, 0:n], start=True, stop=False)
                pe.matmul(bS[q % 2][:, 0:n], g_lo[:, tile], xT[:, 0:n], start=False, stop=False)
                pe.matmul(bS[q % 2][:, q * P:n], ident_b, mask, start=False, stop=True).then_inc(scored.sem, 1)

            def turned_free(b, q):
                if q >= 1:
                    pe.wait_ge(moved.sem, moved.at(b, q))
                elif has(b - 2):
                    pe.wait_ge(scaled.sem, scaled.at(b - 2, 1))
                elif has(b - 1):
                    pe.wait_ge(moved.sem, moved.at(b - 1))

            def turn_probs(b, q):
                pe.wait_ge(exped.sem, exped.at(b, q + 1))
                turned_free(b, q)
                for j in range(q + 1):
                    last = pe.transpose(bX[:, j * P:j * P + P], probs[:, q, j * P:j * P + P], ident)
                last.then_inc(turned.sem, 1)

            def attend(b, q):
                pe.wait_ge(moved.sem, moved.at(b, q + 1))
                if q == 0:
                    pe.wait_ge(v_ready.sem, v_ready.at(b))
                    if has(b - 2):
                        pe.wait_ge(scaled.sem, scaled.at(b - 2, 3))
                    elif has(b - 1):
                        pe.wait_ge(added.sem, added.at(b - 1))
                for j in range(q + 1):
                    last = pe.matmul(o_ps[:, q, :], pT[:, q, j, :], v_sb[:, j, 0:D], start=(j == 0), stop=(j == q))
                last.then_inc(attended.sem, 1)

            def logits(b):
                pe.wait_ge(x2T_sb.sem, x2T_sb.at(b))
                if has(b + 1):
                    pe.wait_ge(v_ready.sem, v_ready.at(b + 1))
                for q in range(Q):
                    tile = x2T[:, q * P:q * P + P]
                    pe.matmul(l_ps[:, q, :], tile, r_hi[:, :], start=True, stop=False)
                    last = pe.matmul(l_ps[:, q, :], tile, r_lo[:, :], start=False, stop=True)
                last.then_inc(routed_ps.sem, 1)

            def turn_weights(b):
                pe.wait_ge(route.sem, route.at(b))
                for q in range(Q):
                    last = pe.transpose(ct_ps[0:KB, q * P:q * P + P],
                                        comb_part[:, q, :, :].rearrange("p n k -> p (n k)"), ident_b)
                last.then_inc(ct_done.sem, 1)

            def first_layer(b, a):
                if a >= 2:
                    pe.wait_ge(gelued.sem, gelued.at(b, a - 1))
                elif has(b + 1):
                    pe.wait_ge(exped.sem, exped.at(b + 1, a + 3))
                elif has(b - 1):
                    pe.wait_ge(gelued.sem, gelued.at(b - 1, a + 3))
                cols = slice(a * P, a * P + P)
                pe.matmul(bS[a % 2][:, :], w1_hi[:, cols], x2T[:, :], start=True, stop=False)
                pe.matmul(bS[a % 2][:, :], w1_lo[:, cols], x2T[:, :], start=False, stop=True)\
                    .then_inc(hidden.sem, 1)

            def spread_weights(b, a):
                if a == 0:
                    pe.wait_ge(ct_ready.sem, ct_ready.at(b))
                elif a == 1 and has(b + 2):
                    pe.wait_ge(xT_sb.sem, xT_sb.at(b + 2))
                elif a == 1:
                    pe.wait_ge(x2T_sb.sem, x2T_sb.at(b))
                elif a == 2 and has(b + 1):
                    pe.wait_ge(added.sem, added.at(b + 1))
                elif a == 3 and has(b + 2):
                    pe.wait_ge(g_lo_sb.sem, g_lo_sb.at(b + 2))
                else:
                    pe.wait_ge(scaled.sem, scaled.at(b - 1, a + 1))
                pe.matmul(w_bank[a][:, :], select[0:KC, a, :], cT[0:KC, :], start=True, stop=True)\
                    .then_inc(spread.sem, 1)

            def second_bias(b):
                if has(b - 1):
                    pe.wait_ge(finished.sem, finished.at(b - 1))
                pe.matmul(bY[0:D, :], b2_rows[:, :], cT[:, :], start=True, stop=False).then_inc(biased.sem, 1)

            def second_layer(b, a):
                pe.wait_ge(scaled.sem, scaled.at(b, a + 1))
                pe.matmul(bY[0:D, :], w2_sb[:, a, :], hs[:, a, :], start=False, stop=(a == PAIRS - 1))\
                    .then_inc(mixed.sem, 1)

            def turn_output(b):
                constant_wait(pe)
                pe.wait_ge(yT_sb.sem, yT_sb.at(b))
                for q in range(Q):
                    last = pe.transpose(y_ps[:, q, :], yT[:, q * P:q * P + P], ident[0:D, 0:D])
                last.then_inc(unmixed.sem, 1)

            def set_up():
                pe.wait_ge(s_cf, 16)
                pe.wait_ge(s_attw, 32)
                for n in range(3):
                    last = pe.transpose(bM[0:D, n * D:n * D + D], wqkv[:, n * D:n * D + D], ident[0:D, 0:D])
                last.then_inc(s_wt_ps, 1)
                pe.wait_ge(s_wt, 1)
                pe.wait_ge(s_prep, PREP_BV)
                pe.wait_ge(s_wp, 32)
                twice = [wT[:, n, :, :].rearrange("d h i -> d (h i)") for n in range(3)]
                pe.matmul(bG[:, 0:P], twice[0], twice[1], start=True, stop=True)
                pe.matmul(bG[:, P:P + 1], twice[1], bcol[:, 0:1], start=True, stop=True)
                pe.matmul(bG[:, 2 * P:2 * P + D], twice[2], wp[:, :], start=True, stop=True)
                pe.matmul(bG[:, 2 * P + D:2 * P + D + 1], twice[0], bcol[:, 1:2], start=True, stop=True)
                pe.matmul(bG[:, 3 * P:3 * P + D], bv_rows[:, :], wp[:, :], start=True, stop=True)
                pe.matmul(bG[:, 3 * P + D:3 * P + D + 1], bq_rows[:, :], bcol[:, 1:2], start=True, stop=True)\
                    .then_inc(s_ab_ps, 1)

            def body(i):
                if has(i):
                    score_tile(i, 0)
                    score_tile(i, 1)
                if has(i - 2):
                    spread_weights(i - 2, 3)
                    second_bias(i - 2)
                    second_layer(i - 2, 0)
                if has(i):
                    turn_probs(i, 0)
                    score_tile(i, 2)
                if has(i - 1):
                    turn_norm(1, i - 1, x2T_ps)
                if has(i):
                    turn_probs(i, 1)
                    score_tile(i, 3)
                if has(i - 2):
                    second_layer(i - 2, 1)
                if has(i):
                    attend(i, 0)
                if peeled(i, 1):
                    pe.wait_ge(s_prep, PREP_ALL)
                if has(i - 1):
                    logits(i - 1)
                if has(i):
                    turn_probs(i, 2)
                if has(i - 1):
                    first_layer(i - 1, 0)
                if has(i):
                    attend(i, 1)
                if has(i - 1):
                    first_layer(i - 1, 1)
                if has(i):
                    turn_probs(i, 3)
                    attend(i, 2)
                if has(i + 1):
                    turn_norm(0, i + 1, xT_ps)
                if has(i - 2):
                    second_layer(i - 2, 2)
                if has(i - 1):
                    turn_weights(i - 1)
                if has(i):
                    attend(i, 3)
                if has(i + 1):
                    project_g(i + 1)
                if has(i - 1):
                    spread_weights(i - 1, 0)
                    first_layer(i - 1, 2)
                    spread_weights(i - 1, 1)
                if has(i - 2):
                    second_layer(i - 2, 3)
                if has(i - 1):
                    first_layer(i - 1, 3)
                if has(i + 1):
                    project_v(i + 1)
                if has(i - 1):
                    spread_weights(i - 1, 2)
                if has(i - 2):
                    turn_output(i - 2)

            set_up()
            pe.wait_ge(s_prep, PREP_ALO)
            turn_norm(0, 0, xT_ps)
            project_g(0)
            pe.wait_ge(s_prep, PREP_WVLO)
            project_v(0)
            pe.wait_ge(s_cb, 1)
            pipeline(pe, body)

        @block.vector
        def _(dve):
            def prep(ins, step):
                ins.then_inc(s_prep, 1)
                dve.wait_ge(s_prep, step)

            def norm_steps(k, b):
                n, mine = ln[k], ln_dve[k]
                constant_wait(dve)
                if k == 0:
                    dve.wait_ge(embedded.sem, embedded.at(b))
                else:
                    dve.wait_ge(added.sem, added.at(b))
                for q in range(Q):
                    last = dve.bn_stats(n["stats"][:, q, :], stream[:, b, q, :])
                last.then_inc(mine.sem, 1)
                yield
                dve.wait_ge(mine.sem, mine.at(b, 1))
                dve.tensor_tensor(n["diff"][:, :], n["stats"][:, :, 1], n["stats"][:, :, 4], ALU.subtract)
                dve.tensor_tensor(n["both"][:, :, :], n["stats"][:, :, 1:3], n["stats"][:, :, 4:6], ALU.add)\
                    .then_inc(mine.sem, 1)
                yield
                dve.wait_ge(mine.sem, mine.at(b, 2))
                dve.scalar_tensor_tensor(out=n["between"][:, :], in0=n["diff"][:, :], scalar=0.25,
                                         in1=n["diff"][:, :], op0=ALU.mult, op1=ALU.mult)
                dve.tensor_scalar(n["within"][:, :], n["both"][:, :, 1], 1.0 / D, EPS, ALU.mult, ALU.add)
                dve.tensor_scalar(n["mean"][:, :], n["both"][:, :, 0], 0.5, None, ALU.mult).then_inc(mine.sem, 1)
                yield
                dve.wait_ge(mine.sem, mine.at(b, 3))
                if has(b - 1):
                    dve.wait_ge(ln_pool[k].sem, ln_pool[k].at(b - 1, 1))
                dve.tensor_tensor(n["var"][:, :], n["between"][:, :], n["within"][:, :], ALU.add)\
                    .then_inc(mine.sem, 1)

            def normalise(k, b):
                n, mine = ln[k], ln_dve[k]
                dve.wait_ge(ln_pool[k].sem, ln_pool[k].at(b, 1))
                if has(b - 1):
                    dve.wait_ge(ln_pool[k].sem, ln_pool[k].at(b - 1))
                    if k == 1:
                        dve.wait_ge(resid.sem, resid.at(b - 1))
                for q in range(Q):
                    last = dve.tensor_scalar(n["xn"][:, q, :], stream[:, b, q, :], n["mean"][:, q:q + 1],
                                             n["rstd"][:, q:q + 1], ALU.subtract, ALU.mult)
                last.then_inc(mine.sem, 1)

            def g_low(b):
                dve.wait_ge(g_hi_sb.sem, g_hi_sb.at(b))
                dve.scalar_tensor_tensor(out=g_lo[:, :], in0=bG[:, :], scalar=c_col[:, 0:1],
                                         in1=g_hi[:, :].bitcast(F32), op0=ALU.add, op1=ALU.subtract)\
                    .then_inc(g_lo_sb.sem, 1)

            def values(b):
                dve.wait_ge(v_done.sem, v_done.at(b))
                dve.tensor_tensor(v_sb[:, :, :], v_ps, v_bias[:, :].unsqueeze(1).to_broadcast([P, Q, VW]),
                                  ALU.add).then_inc(v_ready.sem, 1)

            def maximum(b, q):
                n = (q + 1) * P
                dve.wait_ge(scored.sem, scored.at(b, q + 1))
                dve.tensor_reduce(row_max[:, q:q + 1], bS[q % 2][:, 0:n], AXX, ALU.max, negate=True)\
                    .then_inc(maxed.sem, 1)

            def set_shift(b, q):
                dve.wait_ge(maxed.sem, maxed.at(b, q + 1))
                if q == 0:
                    dve.wait_ge(v_ready.sem, v_ready.at(b))
                    if has(b - 1):
                        dve.wait_ge(exped.sem, exped.at(b - 1))
                dve.tensor_scalar(shift[:, q:q + 1], row_max[:, q:q + 1], v_sb[:, q, D:D + 1], v_sb[:, q, D:D + 1],
                                  ALU.subtract, ALU.add).then_inc(shifted.sem, 1)

            def add_attention(b):
                dve.wait_ge(exped.sem, exped.at(b))
                dve.reciprocal(row_inv[:, :], row_sum[:, :]).then_inc(inverted.sem, 1)
                dve.wait_ge(inverted.sem, inverted.at(b))
                dve.wait_ge(attended.sem, attended.at(b))
                for q in range(Q):
                    last = dve.scalar_tensor_tensor(out=stream[:, b, q, :], in0=o_ps[:, q, :],
                                                    scalar=row_inv[:, q:q + 1], in1=stream[:, b, q, :],
                                                    op0=ALU.mult, op1=ALU.add)
                last.then_inc(added.sem, 1)

            def route_steps(b):
                def done(ins, step):
                    ins.then_inc(route.sem, 1)

                def after(step):
                    dve.wait_ge(route.sem, route.at(b, step))

                def comb_parts(n):
                    return comb_part[:, :, :, n * E:n * E + E]

                rest = comb_rest[:, :, :].unsqueeze(2).to_broadcast([P, Q, SPLIT, E])

                constant_wait(dve)
                dve.wait_ge(routed_ps.sem, routed_ps.at(b))
                for q in range(Q):
                    last = dve.max(top[:, q, :], l_ps[:, q, :])
                done(last, 1)
                yield
                after(1)
                if has(b - 1):
                    dve.wait_ge(route_exp.sem, route_exp.at(b - 1))
                done(dve.tensor_tensor(top_d[:, :, :], top[:, :, :], top[:, :, 0:1].to_broadcast([P, Q, E]),
                                       ALU.subtract), 2)
                for q in range(Q):
                    last = dve.max_index(top_i[:, q, :], top[:, q, :], l_ps[:, q, :])
                done(last, 3)
                yield
                after(3)
                done(dve.tensor_tensor(chosen[:, :, :, :],
                                       top_i[:, :, 0:TOPK].unsqueeze(3).to_broadcast([P, Q, TOPK, E]),
                                       iota.unsqueeze(1).unsqueeze(1).to_broadcast([P, Q, TOPK, E]),
                                       ALU.is_equal), 4)
                yield
                dve.wait_ge(route_exp.sem, route_exp.at(b))
                done(dve.tensor_reduce(esum[:, :, 0], top_e[:, :, :], AXX, ALU.add), 5)
                done(dve.tensor_tensor(pair_sum[:, :, :], top_e[:, :, 0:1], top_e[:, :, 1:2], ALU.add), 6)
                yield
                after(6)
                done(dve.scalar_tensor_tensor(out=denom[:, :, 0], in0=esum[:, :, 0], scalar=GUARD,
                                              in1=pair_sum[:, :, 0], op0=ALU.mult, op1=ALU.max), 7)
                yield
                after(7)
                done(dve.reciprocal(inv[:, :, :], denom[:, :, :]), 8)
                yield
                after(8)
                done(dve.tensor_tensor(weight[:, :, :], top_e[:, :, 0:TOPK],
                                       inv[:, :, :].to_broadcast([P, Q, TOPK]), ALU.mult), 9)
                yield
                after(9)
                done(dve.tensor_tensor(placed[:, :, :, :], chosen[:, :, :, :],
                                       weight[:, :, :].unsqueeze(3).to_broadcast([P, Q, TOPK, E]), ALU.mult), 10)
                yield
                after(10)
                done(dve.tensor_tensor(comb[:, :, :], placed[:, :, 0, :], placed[:, :, 1, :], ALU.add), 11)
                yield
                after(11)
                if has(b - 1):
                    dve.wait_ge(ct_done.sem, ct_done.at(b - 1))
                done(dve.tensor_copy(comb_parts(0), comb[:, :, :].unsqueeze(2).to_broadcast([P, Q, SPLIT, E])), 12)
                yield
                after(12)
                done(dve.tensor_tensor(comb_rest[:, :, :], comb[:, :, :], comb_part[:, :, 0, 0:E],
                                       ALU.subtract), 13)
                yield
                after(13)
                done(dve.tensor_copy(comb_parts(1), rest), 14)
                yield
                after(14)
                done(dve.tensor_tensor(comb_parts(2), rest, comb_parts(1), ALU.subtract), 15)

            def keep_weights(b):
                dve.wait_ge(ct_done.sem, ct_done.at(b))
                if has(b - 1):
                    dve.wait_ge(biased.sem, biased.at(b - 1))
                dve.tensor_copy(cT[:, :], ct_ps[0:KB, :]).then_inc(ct_ready.sem, 1)

            def scale_pair(b, a):
                dve.wait_ge(gelued.sem, gelued.at(b, a + 1))
                dve.wait_ge(spread.sem, spread.at(b, a + 1))
                if has(b - 1):
                    dve.wait_ge(mixed.sem, mixed.at(b - 1, a + 1))
                dve.tensor_tensor(hs[:, a, :], w_bank[a][:, :], hg[:, a, :], ALU.mult)\
                    .then_inc(scaled.sem, 1)

            def finish(b):
                dve.wait_ge(unmixed.sem, unmixed.at(b))
                dve.wait_ge(resid.sem, resid.at(b))
                dve.tensor_tensor(stream[:, b], y_ps, stream[:, b], ALU.add).then_inc(finished.sem, 1)

            def split_weights(hi, lo, full, step):
                prep(dve.tensor_copy(hi, full), step)
                prep(dve.tensor_tensor(lo, full, hi.bitcast(F32), ALU.subtract), step + 1)

            def set_up_attention():
                dve.wait_ge(s_attw, 32)
                prep(dve.tensor_copy(bq_rows[:, :], bcol[:, 0:1].to_broadcast([D, P])), PREP_BQ)
                prep(dve.tensor_copy(bv_rows[:, :], bcol[:, 2:3].to_broadcast([D, P])), PREP_BV)
                dve.wait_ge(s_wt_ps, 1)
                dve.tensor_copy(wT[:, :, :, :], bM[0:D, 0:3 * D].rearrange("d (t i) -> d t i", t=3).unsqueeze(2)
                                .to_broadcast([D, 3, 2, D])).then_inc(s_wt, 1)
                dve.wait_ge(s_ab_ps, 1)
                prep(dve.tensor_scalar(c_col[:, :], bG[:, P:P + 1], SCALE, None, ALU.mult), PREP_C)
                prep(dve.tensor_scalar(a_hi[:, :], bG[:, 0:P], SCALE, None, ALU.mult), PREP_AHI)
                prep(dve.scalar_tensor_tensor(out=a_lo[:, :], in0=bG[:, 0:P], scalar=SCALE,
                                              in1=a_hi[:, :].bitcast(F32), op0=ALU.mult, op1=ALU.subtract), PREP_ALO)
                wv, vb = bG[:, 2 * P:2 * P + D + 1], bG[:, 3 * P:3 * P + D + 1]
                prep(dve.tensor_copy(wv_f[:, 0:D], wv[:, 0:D]), PREP_WV)
                prep(dve.tensor_scalar(wv_f[:, D:D + 1], wv[:, D:D + 1], SCALE, None, ALU.mult), PREP_WU)
                prep(dve.memset(wv_f[:, D + 1:VW], 0.0), PREP_WPAD)
                dve.wait_ge(s_wp, 32)
                prep(dve.tensor_tensor(v_bias[:, 0:D], vb[:, 0:D], bp[:, :], ALU.add), PREP_VB)
                prep(dve.tensor_scalar(v_bias[:, D:D + 1], vb[:, D:D + 1], SCALE, None, ALU.mult), PREP_VK)
                prep(dve.memset(v_bias[:, D + 1:VW], 0.0), PREP_VPAD)
                split_weights(wv_hi[:, :], wv_lo[:, :], wv_f[:, :], PREP_WVHI)

            def set_up_experts():
                dve.wait_ge(s_moew, 16 * 15)
                split_weights(r_hi[:, :], r_lo[:, :], r_f[:, :], PREP_RHI)
                dve.wait_ge(s_w1hi, 1)
                prep(dve.tensor_tensor(w1_lo[:, :], w1_f[:, :], w1_hi[:, :].bitcast(F32), ALU.subtract), PREP_W1LO)
                for n in range(SPLIT):
                    left = b2_f[:, :] if n == 0 else b2_rest[:, n - 1, :]
                    prep(dve.tensor_copy(b2_part[:, n, :], left), PREP_B2 + 3 * n)
                    if n < SPLIT - 1:
                        prep(dve.tensor_tensor(b2_rest[:, n, :], left, b2_part[:, n, :], ALU.subtract),
                             PREP_B2 + 3 * n + 1)
                    rows_n = slice(n * KG, n * KG + KG)
                    prep(dve.tensor_copy(b2_rows[rows_n, :], b2_part[rows_n, n, :]),
                         PREP_B2 + 3 * n + (2 if n < SPLIT - 1 else 1))

            def run(steps_, n=1):
                for _ in range(n):
                    next(steps_, None)

            def body(i):
                norm1 = norm_steps(0, i + 1) if has(i + 1) else iter(())
                norm2 = norm_steps(1, i) if has(i) else iter(())
                routing = route_steps(i - 1) if has(i - 1) else iter(())
                if has(i):
                    maximum(i, 0)
                    maximum(i, 1)
                    set_shift(i, 0)
                    set_shift(i, 1)
                if has(i - 1):
                    normalise(1, i - 1)
                run(norm1, 2)
                if has(i - 2):
                    scale_pair(i - 2, 2)
                if has(i):
                    maximum(i, 2)
                run(norm1)
                if has(i):
                    set_shift(i, 2)
                run(norm1)
                if has(i):
                    maximum(i, 3)
                if has(i - 2):
                    scale_pair(i - 2, 3)
                if has(i):
                    set_shift(i, 3)
                run(routing, 2)
                if has(i + 1):
                    normalise(0, i + 1)
                run(routing, 16)
                if has(i - 1):
                    keep_weights(i - 1)
                if has(i):
                    add_attention(i)
                run(norm2)
                if has(i + 1):
                    g_low(i + 1)
                run(norm2)
                if has(i - 1):
                    scale_pair(i - 1, 0)
                run(norm2)
                if has(i + 1):
                    values(i + 1)
                run(norm2)
                if has(i - 1):
                    scale_pair(i - 1, 1)
                if has(i - 2):
                    finish(i - 2)

            set_up_attention()
            dve.wait_ge(s_zeroed, 2)
            run(norm_steps(0, 0), 4)
            normalise(0, 0)
            g_low(0)
            values(0)
            set_up_experts()
            pipeline(dve, body)


def constants():
    f = np.zeros((P, C_F32), np.float32)
    f[:, C_ID:C_ID + P] = np.eye(P)
    d = np.arange(D)
    exponent = (d - d % 2).astype(np.float32) / np.float32(D)
    inv_freq = np.power(np.float32(10000.0), -exponent)
    angle = np.arange(T, dtype=np.float32)[:, None] * inv_freq
    table = np.where(d % 2 == 0, np.sin(angle), np.cos(angle)).astype(np.float32)
    f[:, C_PE:C_PE + Q * D] = table.reshape(Q, P, D).transpose(1, 0, 2).reshape(P, Q * D)
    f[:, C_IOTA:C_IOTA + E] = np.arange(E)
    b = np.zeros((P, C_BF16), np.float32)
    b[:, C_ID:C_ID + P] = np.eye(P)
    b[:, C_MASK:C_MASK + P] = np.where(np.arange(P)[None, :] > np.arange(P)[:, None], MASKED, 0.0)
    for a in range(PAIRS):
        for part in range(SPLIT):
            for e in range(2):
                at = C_SEL + a * P + e * D
                b[part * E + 2 * a + e, at:at + D] = 1.0
    return f, b


def kernel(x, L0_tok_W, L0_attn_W_qkv, L0_attn_b_qkv, L0_attn_W_proj, L0_attn_b_proj, L0_ffn_router_w,
           L0_ffn_w1, L0_ffn_b1, L0_ffn_w2, L0_ffn_b2):
    import concourse.bacc as bacc
    from concourse.bass_utils import run_bass_kernel_spmd as run

    f, b = constants()
    arrays = {
        "ids": np.ascontiguousarray(np.asarray(x).reshape(B * Q, P).T),
        "table": L0_tok_W, "w_qkv": L0_attn_W_qkv, "b_qkv": np.asarray(L0_attn_b_qkv).reshape(3, D).T, "w_proj": L0_attn_W_proj,
        "b_proj": L0_attn_b_proj, "router": np.asarray(L0_ffn_router_w).T, "w1": L0_ffn_w1, "b1": np.asarray(L0_ffn_b1).reshape(PAIRS, P).T,
        "w2": L0_ffn_w2, "b2": L0_ffn_b2, "const": f, "const_b": b,
    }
    arrays = {name: np.ascontiguousarray(a) for name, a in arrays.items()}
    nc = bacc.Bacc("TRN2", target_bir_lowering=False, num_devices=1)
    aps = {name: nc.dram_tensor(name, a.shape, mybir.dt.from_np(a.dtype), kind="ExternalInput").ap()
           for name, a in arrays.items()}
    out = nc.dram_tensor("out", (B, T, D), F32, kind="ExternalOutput").ap()
    build(nc, **aps, out=out)
    return run(nc, [arrays], core_ids=[0]).results[0]["out"]
```

```python
from contextlib import ExitStack

import numpy as np
import concourse.bass as bass
from concourse import mybir

F32 = mybir.dt.float32
F32R = mybir.dt.float32r
BF16 = mybir.dt.bfloat16
U32 = mybir.dt.uint32
I32 = mybir.dt.int32
ALU = mybir.AluOpType
ACT = mybir.ActivationFunctionType
AXX = mybir.AxisListType.X

B, T, D = 8, 512, 64
E, TOPK = 8, 2
P = 128
Q = T // P
PAIRS = E * D // P
VW = D + 2
SPLIT = 3
KC = SPLIT * E
KG = 32
KB = SPLIT * KG
EPS = 1e-5
SCALE = float(D) ** -0.5
GUARD = 1e-12
MASKED = -1e30

C_ID, C_PE, C_IOTA, C_F32 = 0, P, P + Q * D, P + Q * D + E
C_MASK, C_SEL, C_BF16 = P, 2 * P, 2 * P + PAIRS * P


class Steps:

    def __init__(self, sem, per=1):
        self.sem, self.per = sem, per

    def at(self, batch, step=None):
        return batch * self.per + (self.per if step is None else step)


def build(nc, ids, table, w_qkv, b_qkv, w_proj, b_proj, router, w1, b1, w2, b2, const, const_b, out):
    ctx = ExitStack()
    with ctx:
        def sb(name, shape, dt=F32):
            return ctx.enter_context(nc.sbuf_tensor(name, shape, dt))

        def bank(name):
            return ctx.enter_context(nc.psum_tensor(name, [P, 512], F32))

        def sem(name):
            return ctx.enter_context(nc.semaphore(name))

        def steps(name, per=1):
            return Steps(sem(name), per)

        cf = sb("cf", [P, C_F32])
        cb_f = sb("cb_f", [P, C_BF16])
        cb = sb("cb", [P, C_BF16], BF16)
        ident = cf[:, C_ID:C_ID + P]
        pos = cf[:, C_PE:C_PE + Q * D].rearrange("p (q d) -> p q d", q=Q)
        iota = cf[:, C_IOTA:C_IOTA + E]
        ident_b = cb[:, C_ID:C_ID + P]
        mask = cb[:, C_MASK:C_MASK + P]
        select = cb[:, C_SEL:C_SEL + PAIRS * P].rearrange("k (a m) -> k a m", a=PAIRS)
        idx = sb("idx", [P, B * Q], I32)
        idx_v = idx[:, :].rearrange("p (b q) -> p b q", q=Q)
        ids_now = sb("ids_now", [P, Q], I32)
        rows = sb("rows", [P, Q, D])
        wqkv = sb("wqkv", [D, 3 * D])
        bcol = sb("bcol", [D, 3])
        wp = sb("wp", [D, D])
        bp = sb("bp", [P, D])
        wT = sb("wT", [D, 3, 2, D])
        bq_rows = sb("bq_rows", [D, P])
        bv_rows = sb("bv_rows", [D, P])
        a_hi, a_lo = sb("a_hi", [P, P], F32R), sb("a_lo", [P, P], F32R)
        c_col = sb("c_col", [P, 1])
        wv_f = sb("wv_f", [P, VW])
        wv_hi, wv_lo = sb("wv_hi", [P, VW], F32R), sb("wv_lo", [P, VW], F32R)
        v_bias = sb("v_bias", [P, VW])
        r_f = sb("r_f", [P, E])
        r_hi, r_lo = sb("r_hi", [P, E], F32R), sb("r_lo", [P, E], F32R)
        w1_f = sb("w1_f", [P, E * D])
        w1_hi, w1_lo = sb("w1_hi", [P, E * D], F32R), sb("w1_lo", [P, E * D], F32R)
        b1_col = sb("b1_col", [P, PAIRS])
        w2_sb = sb("w2_sb", [P, PAIRS, D])
        b2_f = sb("b2_f", [KB, D])
        b2_rest = sb("b2_rest", [KB, 2, D])
        b2_part = sb("b2_part", [KB, SPLIT, D], BF16)
        b2_rows = sb("b2_rows", [KB, D], BF16)
        powers = sb("powers", [P, Q + 1])
        warm = sb("warm", [P, 1])

        stream = sb("stream", [P, B, Q, D])
        ln = []
        for k in (1, 2):
            ln.append(dict(
                stats=sb(f"stats{k}", [P, Q, 6]), diff=sb(f"diff{k}", [P, Q]), both=sb(f"both{k}", [P, Q, 2]),
                between=sb(f"between{k}", [P, Q]), within=sb(f"within{k}", [P, Q]), mean=sb(f"mean{k}", [P, Q]),
                var=sb(f"var{k}", [P, Q]), rstd=sb(f"rstd{k}", [P, Q]), xc=sb(f"xc{k}", [P, Q, D]),
                xn=sb(f"xn{k}", [P, Q, D]),
                xs=sb(f"xs{k}", [P, Q, 2, D])))
        xT = sb("xT", [P, T], F32R)
        x2T = sb("x2T", [P, T], F32R)
        g_hi, g_lo = sb("g_hi", [P, T], F32R), sb("g_lo", [P, T], F32R)
        v_sb = sb("v_sb", [P, Q, VW])
        row_max = sb("row_max", [P, Q])
        shift = sb("shift", [P, Q])
        probs = sb("probs", [P, Q, T])
        row_sum = sb("row_sum", [P, Q])
        row_inv = sb("row_inv", [P, Q])
        pT = sb("pT", [P, Q, Q, P])
        top = sb("top", [P, Q, E])
        top_i = sb("top_i", [P, Q, E], U32)
        top_d = sb("top_d", [P, Q, E])
        top_e = sb("top_e", [P, Q, E])
        chosen = sb("chosen", [P, Q, TOPK, E])
        esum = sb("esum", [P, Q, 1])
        pair_sum = sb("pair_sum", [P, Q, 1])
        denom = sb("denom", [P, Q, 1])
        inv = sb("inv", [P, Q, 1])
        placed = sb("placed", [P, Q, TOPK, E])
        comb_e = sb("comb_e", [P, Q, E])
        comb = sb("comb", [P, Q, E])
        comb_rest = sb("comb_rest", [P, Q, E])
        comb_part = sb("comb_part", [P, Q, SPLIT, KG], BF16)
        cT = sb("cT", [KB, T], BF16)
        hg = sb("hg", [P, PAIRS, T])
        hs = sb("hs", [P, PAIRS, T])
        yT = sb("yT", [D, T])

        bT = bank("bT")
        bG = bank("bG")
        bM = bank("bM")
        bS = [bank("bS0"), bank("bS1")]
        bX = bank("bX")
        bO = bank("bO")
        bY = bank("bY")
        v_ps = bM[:, 0:Q * VW].rearrange("p (q n) -> p q n", q=Q)
        l_ps = bM[:, Q * VW:Q * VW + Q * E].rearrange("p (q e) -> p q e", q=Q)
        ct_ps = bM[:, 0:T // 2].bitcast(BF16)
        o_ps = bO[:, 0:Q * D].rearrange("p (q d) -> p q d", q=Q)
        y_ps = bY[:, 0:Q * D].rearrange("p (q d) -> p q d", q=Q)
        w_bank = [bX, bT, bO, bG]

        s_idx, s_cf, s_cbf, s_cb = sem("s_idx"), sem("s_cf"), sem("s_cbf"), sem("s_cb")
        s_attw, s_wp, s_moew = sem("s_attw"), sem("s_wp"), sem("s_moew")
        s_half = sem("s_half")
        s_zeroed = sem("s_zeroed")
        s_wt_ps, s_wt, s_ab_ps = sem("s_wt_ps"), sem("s_wt"), sem("s_ab_ps")
        s_prep = sem("s_prep")
        s_w1hi = sem("s_w1hi")
        picked = steps("picked")
        gathered = steps("gathered", 16 * Q)
        embedded = steps("embedded")
        ln_dve = [steps("ln1_dve", 6), steps("ln2_dve", 6)]
        ln_pool = [steps("ln1_pool", 3), steps("ln2_pool", 3)]
        resid = steps("resid")
        xT_ps, xT_sb = steps("xT_ps"), steps("xT_sb")
        x2T_ps, x2T_sb = steps("x2T_ps"), steps("x2T_sb")
        g_ps, g_hi_sb, g_lo_sb = steps("g_ps"), steps("g_hi_sb"), steps("g_lo_sb")
        v_done, v_ready = steps("v_done"), steps("v_ready")
        scored = steps("scored", Q)
        maxed = steps("maxed", Q)
        shifted = steps("shifted", Q)
        exped = steps("exped", Q)
        turned = steps("turned", Q)
        moved = steps("moved", Q)
        attended = steps("attended", Q)
        inverted = steps("inverted")
        added = steps("added")
        routed_ps = steps("routed_ps")
        route = steps("route", 15)
        route_exp = steps("route_exp")
        ct_done, ct_ready = steps("ct_done"), steps("ct_ready")
        hidden = steps("hidden", PAIRS)
        spread = steps("spread", PAIRS)
        gelued = steps("gelued", PAIRS)
        scaled = steps("scaled", PAIRS)
        biased = steps("biased")
        mixed = steps("mixed", PAIRS)
        yT_sb = steps("yT_sb")
        unmixed = steps("unmixed")
        finished = steps("finished")
        s_store = sem("s_store")

        (PREP_BQ, PREP_BV, PREP_AHI, PREP_C, PREP_WV, PREP_WU, PREP_WPAD, PREP_ALO, PREP_WVHI, PREP_VB, PREP_VK,
         PREP_VPAD, PREP_WVLO, PREP_RHI, PREP_B2) = range(1, 16)
        PREP_ALL = PREP_B2 + 6 + SPLIT

        def has(batch):
            return not isinstance(batch, int) or 0 <= batch < B

        def peeled(i, n):
            return isinstance(i, int) and i == n

        def constant_wait(eng):
            eng.wait_ge(s_idx, 16)

        def pipeline(eng, body, tail):
            for i in (0, 1, 2):
                body(i)
            with eng.Fori(3, B - 1) as i:
                body(i)
            body(B - 1)
            tail(B - 2, B - 1)

        block = ctx.enter_context(nc.Block())

        @block.sync
        def _(sp):
            sp.dma_start(idx[:, :], ids).then_inc(s_idx, 16)
            sp.dma_start(cf[:, :], const).then_inc(s_cf, 16)
            sp.dma_start(wp[:, :], w_proj).then_inc(s_wp, 16)
            sp.dma_start(bp[:, :], b_proj.partition_broadcast(P)).then_inc(s_wp, 16)
            for half in range(2):
                rows = slice(half * D, half * D + D)
                sp.dma_start(w1_f[rows, :].rearrange("i (e f) -> i e f", e=E),
                             w1.rearrange("e i f -> i e f")).then_inc(s_moew, 16)
                sp.dma_start(r_f[rows, :], router).then_inc(s_moew, 16)
            sp.dma_start(w2_sb[:, :, :], w2.rearrange("(a e) f d -> (e f) a d", e=2)).then_inc(s_moew, 16)
            sp.dma_start(b1_col[:, :], b1).then_inc(s_moew, 16)
            sp.wait_ge(s_zeroed, 2)
            for part in range(SPLIT):
                for copy in range(SPLIT):
                    at = copy * KG + part * E
                    sp.dma_start(b2_f[at:at + E, :], b2).then_inc(s_moew, 16)

            out_v = out.rearrange("b (q p) d -> b p q d", q=Q)
            with sp.Fori(0, B) as b:
                sp.wait_ge(finished.sem, finished.at(b))
                sp.dma_start(out_v[b], stream[:, b]).then_inc(s_store, 16)
            sp.wait_ge(s_store, 16 * B)

        @block.gpsimd
        def _(pool):
            def pick(b):
                pool.tensor_copy(ids_now[:, :], idx_v[:, b, :]).then_inc(picked.sem, 1)

            def gather(b):
                for q in range(Q):
                    pool.indirect_dma_start(
                        out=rows[:, q, :], out_offset=None, in_=table,
                        in_offset=bass.IndirectOffsetOnAxis(ap=ids_now[:, q:q + 1], axis=0),
                        bounds_check=table.shape[0] - 1).then_inc(gathered.sem, 16)

            def embed(b):
                pool.wait_ge(gathered.sem, gathered.at(b))
                pool.tensor_tensor(stream[:, b], rows[:, :, :], pos, ALU.add).then_inc(embedded.sem, 1)

            def may_gather(b):
                pool.wait_ge(picked.sem, picked.at(b))
                pool.wait_ge(embedded.sem, embedded.at(b - 1))

            def inverse_deviation(k, b):
                n, mine, dve = ln[k], ln_pool[k], ln_dve[k]
                pool.wait_ge(dve.sem, dve.at(b, 4))
                pool.tensor_tensor(n["rstd"][:, :], n["var"][:, :], powers[:, 0:Q], ALU.pow).then_inc(mine.sem, 1)

            def split(k, b, read):
                n, mine, dve = ln[k], ln_pool[k], ln_dve[k]
                pool.wait_ge(dve.sem, dve.at(b))
                if has(b - 1):
                    pool.wait_ge(read.sem, read.at(b - 1))
                pool.tensor_tensor(n["xs"][:, :, 0, :].bitcast(F32R), n["xn"][:, :, :],
                                   powers[:, Q:Q + 1].unsqueeze(2).to_broadcast([P, Q, D]), ALU.add)\
                    .then_inc(mine.sem, 1)
                pool.wait_ge(mine.sem, mine.at(b, 2))
                pool.tensor_tensor(n["xs"][:, :, 1, :], n["xn"][:, :, :], n["xs"][:, :, 0, :], ALU.subtract)\
                    .then_inc(mine.sem, 1)

            def add_norm2(b):
                pool.tensor_tensor(stream[:, b], stream[:, b], ln[1]["xn"][:, :, :], ALU.add).then_inc(resid.sem, 1)

            pool.memset(powers[:, 0:Q], -0.5).then_inc(s_half, 1)
            pool.memset(powers[:, Q:Q + 1], 0.0).then_inc(s_half, 1)
            pool.memset(comb_part[:, :, :, :], 0.0).then_inc(s_zeroed, 1)
            pool.memset(b2_f[:, :], 0.0).then_inc(s_zeroed, 1)
            pool.wait_ge(s_idx, 16)
            pick(0)
            pool.wait_ge(picked.sem, picked.at(0))
            gather(0)
            pool.wait_ge(s_half, 2)
            pool.wait_ge(s_cf, 16)
            embed(0)

            def body(i):
                if has(i + 1):
                    inverse_deviation(0, i + 1)
                if has(i + 2):
                    pick(i + 2)
                if has(i + 1):
                    split(0, i + 1, xT_ps)
                if has(i + 2):
                    gather(i + 2)
                    may_gather(i + 2)
                    embed(i + 2)
                if has(i):
                    inverse_deviation(1, i)
                    split(1, i, x2T_ps)
                    add_norm2(i)

            for i in (-1, 0, 1):
                body(i)
            with pool.Fori(2, B - 2) as i:
                body(i)
            for i in (B - 2, B - 1):
                body(i)

        @block.scalar
        def _(act):
            act.dma_start(wqkv[:, :], w_qkv).then_inc(s_attw, 16)
            act.dma_start(bcol[:, :], b_qkv).then_inc(s_attw, 16)
            act.dma_start(cb_f[:, :], const_b).then_inc(s_cbf, 16)
            act.wait_ge(s_cbf, 16)
            act.activation(cb[:, :], cb_f[:, :], ACT.Copy).then_inc(s_cb, 1)
            act.wait_ge(s_moew, 16 * 15)
            act.activation(w1_hi[:, :], w1_f[:, :], ACT.Copy).then_inc(s_w1hi, 1)

            def to_sbuf_1(b):
                act.wait_ge(xT_ps.sem, xT_ps.at(b))
                if has(b - 1):
                    act.wait_ge(scored.sem, scored.at(b - 1))
                    act.wait_ge(v_done.sem, v_done.at(b - 1))
                act.activation(xT[:, :], bT[:, :], ACT.Copy).then_inc(xT_sb.sem, 1)

            def to_sbuf_2(b):
                act.wait_ge(x2T_ps.sem, x2T_ps.at(b))
                if has(b - 1):
                    act.wait_ge(hidden.sem, hidden.at(b - 1))
                act.activation(x2T[:, :], bT[:, :], ACT.Copy).then_inc(x2T_sb.sem, 1)

            def exp_tile(b, q):
                n = (q + 1) * P
                act.wait_ge(shifted.sem, shifted.at(b, q + 1))
                if has(b - 1):
                    act.wait_ge(turned.sem, turned.at(b - 1, q + 1))
                    act.wait_ge(inverted.sem, inverted.at(b - 1))
                act.activation(probs[:, q, 0:n], bS[q % 2][:, 0:n], ACT.Exp, bias=shift[:, q:q + 1],
                               accum_out=row_sum[:, q:q + 1]).then_inc(exped.sem, 1)

            def move_turned(b, q):
                act.wait_ge(turned.sem, turned.at(b, q + 1))
                if has(b - 1):
                    act.wait_ge(attended.sem, attended.at(b - 1, q + 1))
                act.activation(pT[:, q, 0:q + 1, :], bX[:, 0:(q + 1) * P].rearrange("p (j t) -> p j t", t=P),
                               ACT.Copy).then_inc(moved.sem, 1)

            def gelu_pair(b, a):
                act.wait_ge(hidden.sem, hidden.at(b, a + 1))
                if has(b - 1):
                    act.wait_ge(scaled.sem, scaled.at(b - 1, a + 1))
                act.activation(hg[:, a, :], bS[a % 2][:, :], ACT.Gelu, bias=b1_col[:, a:a + 1])\
                    .then_inc(gelued.sem, 1)

            def keep_output(b):
                act.wait_ge(mixed.sem, mixed.at(b))
                if has(b - 1):
                    act.wait_ge(unmixed.sem, unmixed.at(b - 1))
                act.activation(yT[:, :], bY[0:D, :], ACT.Copy).then_inc(yT_sb.sem, 1)

            def route_exp_of(b):
                act.wait_ge(route.sem, route.at(b, 2))
                act.activation(top_e[:, :, :], top_d[:, :, :], ACT.Exp).then_inc(route_exp.sem, 1)

            def load_function(func):
                act.activation(warm[:, :], powers[:, Q:Q + 1], func)

            def g_high(b):
                act.wait_ge(g_ps.sem, g_ps.at(b))
                act.activation(g_hi[:, :], bG[:, :], ACT.Identity, bias=c_col[:, 0:1]).then_inc(g_hi_sb.sem, 1)

            def body(i):
                if has(i):
                    exp_tile(i, 0)
                    move_turned(i, 0)
                    exp_tile(i, 1)
                if has(i - 1):
                    to_sbuf_2(i - 1)
                if has(i):
                    exp_tile(i, 2)
                    move_turned(i, 1)
                    exp_tile(i, 3)
                    move_turned(i, 2)
                if has(i - 1):
                    route_exp_of(i - 1)
                if has(i):
                    move_turned(i, 3)
                if has(i - 1):
                    load_function(ACT.Gelu)
                if has(i + 1):
                    to_sbuf_1(i + 1)
                if has(i - 1):
                    gelu_pair(i - 1, 0)
                if has(i + 1):
                    g_high(i + 1)
                if has(i - 1):
                    gelu_pair(i - 1, 1)
                if has(i - 2):
                    keep_output(i - 2)
                if has(i - 1):
                    gelu_pair(i - 1, 2)
                    gelu_pair(i - 1, 3)
                if not peeled(i, 0):
                    load_function(ACT.Exp)

            act.wait_ge(s_half, 2)
            to_sbuf_1(0)
            act.wait_ge(s_prep, PREP_C)
            g_high(0)

            def tail(x, y):
                to_sbuf_2(y)
                route_exp_of(y)
                gelu_pair(y, 0)
                load_function(ACT.Gelu)
                keep_output(x)
                gelu_pair(y, 1)
                gelu_pair(y, 2)
                gelu_pair(y, 3)
                keep_output(y)

            pipeline(act, body, tail)

        @block.tensor
        def _(pe):
            def turn_norm(k, b, done):
                pe.wait_ge(ln_pool[k].sem, ln_pool[k].at(b))
                if k == 0 and has(b - 2):
                    pe.wait_ge(x2T_sb.sem, x2T_sb.at(b - 2))
                elif k == 0 and has(b - 1):
                    pe.wait_ge(xT_sb.sem, xT_sb.at(b - 1))
                elif k == 1 and has(b - 1):
                    pe.wait_ge(scaled.sem, scaled.at(b - 1, 2))
                elif k == 1:
                    pe.wait_ge(xT_sb.sem, xT_sb.at(b + 1))
                for q in range(Q):
                    last = pe.transpose(bT[:, q * P:q * P + P],
                                        ln[k]["xs"][:, q, :, :].rearrange("p h d -> p (h d)"), ident)
                last.then_inc(done.sem, 1)

            def project_g(b):
                if has(b - 3):
                    pe.wait_ge(scaled.sem, scaled.at(b - 3))
                pe.wait_ge(xT_sb.sem, xT_sb.at(b))
                if has(b - 1):
                    pe.wait_ge(g_lo_sb.sem, g_lo_sb.at(b - 1))
                pe.matmul(bG[:, :], a_hi[:, :], xT[:, :], start=True, stop=False)
                pe.matmul(bG[:, :], a_lo[:, :], xT[:, :], start=False, stop=True).then_inc(g_ps.sem, 1)

            def project_v(b):
                if has(b - 2):
                    pe.wait_ge(ct_ready.sem, ct_ready.at(b - 2))
                for q in range(Q):
                    tile = xT[:, q * P:q * P + P]
                    pe.matmul(v_ps[:, q, :], tile, wv_hi[:, :], start=True, stop=False)
                    last = pe.matmul(v_ps[:, q, :], tile, wv_lo[:, :], start=False, stop=True)
                last.then_inc(v_done.sem, 1)

            def score_tile(b, q):
                n = (q + 1) * P
                if q == 0:
                    pe.wait_ge(g_lo_sb.sem, g_lo_sb.at(b))
                if q >= 2:
                    pe.wait_ge(exped.sem, exped.at(b, q - 1))
                elif has(b - 2):
                    pe.wait_ge(gelued.sem, gelued.at(b - 2, q + 3))
                elif has(b - 1):
                    pe.wait_ge(exped.sem, exped.at(b - 1, q + 3))
                tile = slice(q * P, q * P + P)
                pe.matmul(bS[q % 2][:, 0:n], g_hi[:, tile], xT[:, 0:n], start=True, stop=False)
                pe.matmul(bS[q % 2][:, 0:n], g_lo[:, tile], xT[:, 0:n], start=False, stop=False)
                pe.matmul(bS[q % 2][:, q * P:n], ident_b, mask, start=False, stop=True).then_inc(scored.sem, 1)

            def turned_free(b, q):
                if q >= 1:
                    pe.wait_ge(moved.sem, moved.at(b, q))
                elif has(b - 2):
                    pe.wait_ge(scaled.sem, scaled.at(b - 2, 1))
                elif has(b - 1):
                    pe.wait_ge(moved.sem, moved.at(b - 1))

            def turn_probs(b, q):
                pe.wait_ge(exped.sem, exped.at(b, q + 1))
                turned_free(b, q)
                for j in range(q + 1):
                    last = pe.transpose(bX[:, j * P:j * P + P], probs[:, q, j * P:j * P + P], ident)
                last.then_inc(turned.sem, 1)

            def attend(b, q):
                pe.wait_ge(moved.sem, moved.at(b, q + 1))
                if q == 0:
                    pe.wait_ge(v_ready.sem, v_ready.at(b))
                    if has(b - 2):
                        pe.wait_ge(scaled.sem, scaled.at(b - 2, 3))
                    elif has(b - 1):
                        pe.wait_ge(added.sem, added.at(b - 1))
                for j in range(q + 1):
                    last = pe.matmul(o_ps[:, q, :], pT[:, q, j, :], v_sb[:, j, 0:D], start=(j == 0), stop=(j == q))
                last.then_inc(attended.sem, 1)

            def logits(b):
                pe.wait_ge(x2T_sb.sem, x2T_sb.at(b))
                if has(b + 1):
                    pe.wait_ge(v_ready.sem, v_ready.at(b + 1))
                for q in range(Q):
                    tile = x2T[:, q * P:q * P + P]
                    pe.matmul(l_ps[:, q, :], tile, r_hi[:, :], start=True, stop=False)
                    last = pe.matmul(l_ps[:, q, :], tile, r_lo[:, :], start=False, stop=True)
                last.then_inc(routed_ps.sem, 1)

            def turn_weights(b):
                pe.wait_ge(route.sem, route.at(b))
                for q in range(Q):
                    last = pe.transpose(ct_ps[0:KB, q * P:q * P + P],
                                        comb_part[:, q, :, :].rearrange("p n k -> p (n k)"), ident_b)
                last.then_inc(ct_done.sem, 1)

            def first_layer(b, a):
                if a >= 2:
                    pe.wait_ge(gelued.sem, gelued.at(b, a - 1))
                elif has(b + 1):
                    pe.wait_ge(exped.sem, exped.at(b + 1, a + 3))
                elif has(b - 1):
                    pe.wait_ge(gelued.sem, gelued.at(b - 1, a + 3))
                cols = slice(a * P, a * P + P)
                pe.matmul(bS[a % 2][:, :], w1_hi[:, cols], x2T[:, :], start=True, stop=False)
                pe.matmul(bS[a % 2][:, :], w1_lo[:, cols], x2T[:, :], start=False, stop=True)\
                    .then_inc(hidden.sem, 1)

            def spread_weights(b, a):
                if a == 0:
                    pe.wait_ge(ct_ready.sem, ct_ready.at(b))
                elif a == 1 and has(b + 2):
                    pe.wait_ge(xT_sb.sem, xT_sb.at(b + 2))
                elif a == 1:
                    pe.wait_ge(x2T_sb.sem, x2T_sb.at(b))
                elif a == 2 and has(b + 1):
                    pe.wait_ge(added.sem, added.at(b + 1))
                elif a == 3 and has(b + 2):
                    pe.wait_ge(g_lo_sb.sem, g_lo_sb.at(b + 2))
                else:
                    pe.wait_ge(scaled.sem, scaled.at(b - 1, a + 1))
                pe.matmul(w_bank[a][:, :], select[0:KC, a, :], cT[0:KC, :], start=True, stop=True)\
                    .then_inc(spread.sem, 1)

            def second_bias(b):
                if has(b - 1):
                    pe.wait_ge(finished.sem, finished.at(b - 1))
                pe.matmul(bY[0:D, :], b2_rows[:, :], cT[:, :], start=True, stop=False).then_inc(biased.sem, 1)

            def second_layer(b, a):
                pe.wait_ge(scaled.sem, scaled.at(b, a + 1))
                pe.matmul(bY[0:D, :], w2_sb[:, a, :], hs[:, a, :], start=False, stop=(a == PAIRS - 1))\
                    .then_inc(mixed.sem, 1)

            def turn_output(b):
                constant_wait(pe)
                pe.wait_ge(yT_sb.sem, yT_sb.at(b))
                for q in range(Q):
                    last = pe.transpose(y_ps[:, q, :], yT[:, q * P:q * P + P], ident[0:D, 0:D])
                last.then_inc(unmixed.sem, 1)

            def set_up():
                pe.wait_ge(s_cf, 16)
                pe.wait_ge(s_attw, 32)
                for n in range(3):
                    last = pe.transpose(bM[0:D, n * D:n * D + D], wqkv[:, n * D:n * D + D], ident[0:D, 0:D])
                last.then_inc(s_wt_ps, 1)
                pe.wait_ge(s_wt, 1)
                pe.wait_ge(s_prep, PREP_BV)
                pe.wait_ge(s_wp, 32)
                twice = [wT[:, n, :, :].rearrange("d h i -> d (h i)") for n in range(3)]
                pe.matmul(bG[:, 0:P], twice[0], twice[1], start=True, stop=True)
                pe.matmul(bG[:, P:P + 1], twice[1], bcol[:, 0:1], start=True, stop=True)
                pe.matmul(bG[:, 2 * P:2 * P + D], twice[2], wp[:, :], start=True, stop=True)
                pe.matmul(bG[:, 2 * P + D:2 * P + D + 1], twice[0], bcol[:, 1:2], start=True, stop=True)
                pe.matmul(bG[:, 3 * P:3 * P + D], bv_rows[:, :], wp[:, :], start=True, stop=True)
                pe.matmul(bG[:, 3 * P + D:3 * P + D + 1], bq_rows[:, :], bcol[:, 1:2], start=True, stop=True)\
                    .then_inc(s_ab_ps, 1)

            def body(i):
                if has(i):
                    score_tile(i, 0)
                    score_tile(i, 1)
                if has(i - 2):
                    spread_weights(i - 2, 3)
                    second_bias(i - 2)
                    second_layer(i - 2, 0)
                if has(i):
                    turn_probs(i, 0)
                    score_tile(i, 2)
                if has(i - 2):
                    second_layer(i - 2, 1)
                if has(i - 1):
                    turn_norm(1, i - 1, x2T_ps)
                if has(i):
                    score_tile(i, 3)
                    turn_probs(i, 1)
                    attend(i, 0)
                if peeled(i, 1):
                    pe.wait_ge(s_prep, PREP_ALL)
                if has(i - 1):
                    logits(i - 1)
                if has(i):
                    turn_probs(i, 2)
                if has(i - 1):
                    first_layer(i - 1, 0)
                if has(i):
                    attend(i, 1)
                    turn_probs(i, 3)
                if has(i - 1):
                    first_layer(i - 1, 1)
                if has(i):
                    attend(i, 2)
                if has(i + 1):
                    turn_norm(0, i + 1, xT_ps)
                if has(i):
                    attend(i, 3)
                if has(i - 1):
                    turn_weights(i - 1)
                if has(i - 2):
                    second_layer(i - 2, 2)
                if has(i + 1):
                    project_g(i + 1)
                if has(i - 2):
                    second_layer(i - 2, 3)
                if has(i - 1):
                    spread_weights(i - 1, 0)
                    first_layer(i - 1, 2)
                    spread_weights(i - 1, 1)
                    first_layer(i - 1, 3)
                if has(i - 2):
                    turn_output(i - 2)
                if has(i + 1):
                    project_v(i + 1)
                if has(i - 1):
                    spread_weights(i - 1, 2)

            set_up()
            pe.wait_ge(s_prep, PREP_ALO)
            turn_norm(0, 0, xT_ps)
            project_g(0)
            pe.wait_ge(s_prep, PREP_WVLO)
            project_v(0)
            pe.wait_ge(s_cb, 1)

            def tail(x, y):
                second_bias(x)
                second_layer(x, 0)
                spread_weights(x, 3)
                turn_norm(1, y, x2T_ps)
                second_layer(x, 1)
                logits(y)
                first_layer(y, 0)
                first_layer(y, 1)
                second_layer(x, 2)
                second_layer(x, 3)
                turn_weights(y)
                first_layer(y, 2)
                turn_output(x)
                spread_weights(y, 0)
                spread_weights(y, 1)
                spread_weights(y, 2)
                first_layer(y, 3)
                spread_weights(y, 3)
                second_bias(y)
                second_layer(y, 0)
                second_layer(y, 1)
                second_layer(y, 2)
                second_layer(y, 3)
                turn_output(y)

            pipeline(pe, body, tail)

        @block.vector
        def _(dve):
            def prep(ins):
                ins.then_inc(s_prep, 1)

            def prepared(step):
                dve.wait_ge(s_prep, step)

            def norm_steps(k, b):
                n, mine = ln[k], ln_dve[k]
                constant_wait(dve)
                if k == 0:
                    dve.wait_ge(embedded.sem, embedded.at(b))
                else:
                    dve.wait_ge(added.sem, added.at(b))
                for q in range(Q):
                    last = dve.bn_stats(n["stats"][:, q, :], stream[:, b, q, :])
                last.then_inc(mine.sem, 1)
                yield
                dve.wait_ge(mine.sem, mine.at(b, 1))
                dve.tensor_tensor(n["diff"][:, :], n["stats"][:, :, 1], n["stats"][:, :, 4], ALU.subtract)
                dve.tensor_tensor(n["both"][:, :, :], n["stats"][:, :, 1:3], n["stats"][:, :, 4:6], ALU.add)\
                    .then_inc(mine.sem, 1)
                yield
                dve.wait_ge(mine.sem, mine.at(b, 2))
                dve.scalar_tensor_tensor(out=n["between"][:, :], in0=n["diff"][:, :], scalar=0.25,
                                         in1=n["diff"][:, :], op0=ALU.mult, op1=ALU.mult)
                dve.tensor_scalar(n["within"][:, :], n["both"][:, :, 1], 1.0 / D, EPS, ALU.mult, ALU.add)
                dve.tensor_scalar(n["mean"][:, :], n["both"][:, :, 0], 0.5, None, ALU.mult).then_inc(mine.sem, 1)
                yield
                dve.wait_ge(mine.sem, mine.at(b, 3))
                if has(b - 1):
                    dve.wait_ge(ln_pool[k].sem, ln_pool[k].at(b - 1, 1))
                dve.tensor_tensor(n["var"][:, :], n["between"][:, :], n["within"][:, :], ALU.add)\
                    .then_inc(mine.sem, 1)
                yield
                dve.tensor_tensor(n["xc"][:, :, :], stream[:, b], n["mean"][:, :].unsqueeze(2).to_broadcast([P, Q, D]),
                                  ALU.subtract).then_inc(mine.sem, 1)

            def normalise(k, b):
                n, mine = ln[k], ln_dve[k]
                dve.wait_ge(ln_pool[k].sem, ln_pool[k].at(b, 1))
                if has(b - 1):
                    dve.wait_ge(ln_pool[k].sem, ln_pool[k].at(b - 1))
                    if k == 1:
                        dve.wait_ge(resid.sem, resid.at(b - 1))
                dve.wait_ge(mine.sem, mine.at(b, 5))
                dve.tensor_tensor(n["xn"][:, :, :], n["xc"][:, :, :],
                                  n["rstd"][:, :].unsqueeze(2).to_broadcast([P, Q, D]), ALU.mult).then_inc(mine.sem, 1)

            def g_low(b):
                dve.wait_ge(g_hi_sb.sem, g_hi_sb.at(b))
                dve.scalar_tensor_tensor(out=g_lo[:, :], in0=bG[:, :], scalar=c_col[:, 0:1],
                                         in1=g_hi[:, :].bitcast(F32), op0=ALU.add, op1=ALU.subtract)\
                    .then_inc(g_lo_sb.sem, 1)

            def values(b):
                dve.wait_ge(v_done.sem, v_done.at(b))
                dve.tensor_tensor(v_sb[:, :, :], v_ps, v_bias[:, :].unsqueeze(1).to_broadcast([P, Q, VW]),
                                  ALU.add).then_inc(v_ready.sem, 1)

            def maximum(b, q):
                n = (q + 1) * P
                dve.wait_ge(scored.sem, scored.at(b, q + 1))
                dve.tensor_reduce(row_max[:, q:q + 1], bS[q % 2][:, 0:n], AXX, ALU.max, negate=True)\
                    .then_inc(maxed.sem, 1)

            def set_shift(b, q):
                dve.wait_ge(maxed.sem, maxed.at(b, q + 1))
                if q == 0:
                    dve.wait_ge(v_ready.sem, v_ready.at(b))
                    if has(b - 1):
                        dve.wait_ge(exped.sem, exped.at(b - 1))
                dve.scalar_tensor_tensor(out=shift[:, q:q + 1], in0=row_max[:, q:q + 1], scalar=v_sb[:, q, D:D + 1],
                                         in1=v_sb[:, q, D:D + 1], op0=ALU.subtract, op1=ALU.add).then_inc(shifted.sem, 1)

            def add_attention(b):
                dve.wait_ge(exped.sem, exped.at(b))
                dve.reciprocal(row_inv[:, :], row_sum[:, :]).then_inc(inverted.sem, 1)
                dve.wait_ge(inverted.sem, inverted.at(b))
                dve.wait_ge(attended.sem, attended.at(b))
                for q in range(Q):
                    last = dve.scalar_tensor_tensor(out=stream[:, b, q, :], in0=o_ps[:, q, :],
                                                    scalar=row_inv[:, q:q + 1], in1=stream[:, b, q, :],
                                                    op0=ALU.mult, op1=ALU.add)
                last.then_inc(added.sem, 1)

            def route_steps(b):
                def done(ins, step):
                    ins.then_inc(route.sem, 1)

                def after(step):
                    dve.wait_ge(route.sem, route.at(b, step))

                def comb_parts(n):
                    return comb_part[:, :, :, n * E:n * E + E]

                rest = comb_rest[:, :, :].unsqueeze(2).to_broadcast([P, Q, SPLIT, E])

                constant_wait(dve)
                dve.wait_ge(routed_ps.sem, routed_ps.at(b))
                for q in range(Q):
                    last = dve.max(top[:, q, :], l_ps[:, q, :])
                done(last, 1)
                yield
                after(1)
                if has(b - 1):
                    dve.wait_ge(route_exp.sem, route_exp.at(b - 1))
                done(dve.tensor_tensor(top_d[:, :, :], top[:, :, :], top[:, :, 0:1].to_broadcast([P, Q, E]),
                                       ALU.subtract), 2)
                for q in range(Q):
                    last = dve.max_index(top_i[:, q, :], top[:, q, :], l_ps[:, q, :])
                done(last, 3)
                yield
                after(3)
                done(dve.tensor_tensor(chosen[:, :, :, :],
                                       top_i[:, :, 0:TOPK].unsqueeze(3).to_broadcast([P, Q, TOPK, E]),
                                       iota.unsqueeze(1).unsqueeze(1).to_broadcast([P, Q, TOPK, E]),
                                       ALU.is_equal), 4)
                yield
                dve.wait_ge(route_exp.sem, route_exp.at(b))
                done(dve.tensor_reduce(esum[:, :, 0], top_e[:, :, :], AXX, ALU.add), 5)
                done(dve.tensor_tensor(pair_sum[:, :, :], top_e[:, :, 0:1], top_e[:, :, 1:2], ALU.add), 6)
                yield
                after(4)
                done(dve.tensor_tensor(placed[:, :, :, :], chosen[:, :, :, :],
                                       top_e[:, :, 0:TOPK].unsqueeze(3).to_broadcast([P, Q, TOPK, E]), ALU.mult), 7)
                yield
                after(6)
                done(dve.scalar_tensor_tensor(out=denom[:, :, 0], in0=esum[:, :, 0], scalar=GUARD,
                                              in1=pair_sum[:, :, 0], op0=ALU.mult, op1=ALU.max), 8)
                yield
                after(7)
                done(dve.tensor_tensor(comb_e[:, :, :], placed[:, :, 0, :], placed[:, :, 1, :], ALU.add), 9)
                yield
                after(8)
                done(dve.reciprocal(inv[:, :, :], denom[:, :, :]), 10)
                yield
                after(10)
                done(dve.tensor_tensor(comb[:, :, :], comb_e[:, :, :], inv[:, :, :].to_broadcast([P, Q, E]),
                                       ALU.mult), 11)
                yield
                after(11)
                if has(b - 1):
                    dve.wait_ge(ct_done.sem, ct_done.at(b - 1))
                done(dve.tensor_copy(comb_parts(0), comb[:, :, :].unsqueeze(2).to_broadcast([P, Q, SPLIT, E])), 12)
                yield
                after(12)
                done(dve.tensor_tensor(comb_rest[:, :, :], comb[:, :, :], comb_part[:, :, 0, 0:E],
                                       ALU.subtract), 13)
                yield
                after(13)
                done(dve.tensor_copy(comb_parts(1), rest), 14)
                yield
                after(14)
                done(dve.tensor_tensor(comb_parts(2), rest, comb_parts(1), ALU.subtract), 15)

            def keep_weights(b):
                dve.wait_ge(ct_done.sem, ct_done.at(b))
                if has(b - 1):
                    dve.wait_ge(biased.sem, biased.at(b - 1))
                dve.tensor_copy(cT[:, :], ct_ps[0:KB, :]).then_inc(ct_ready.sem, 1)

            def scale_pair(b, a):
                dve.wait_ge(gelued.sem, gelued.at(b, a + 1))
                dve.wait_ge(spread.sem, spread.at(b, a + 1))
                if has(b - 1):
                    dve.wait_ge(mixed.sem, mixed.at(b - 1, a + 1))
                dve.tensor_tensor(hs[:, a, :], w_bank[a][:, :], hg[:, a, :], ALU.mult)\
                    .then_inc(scaled.sem, 1)

            def finish(b):
                dve.wait_ge(unmixed.sem, unmixed.at(b))
                dve.wait_ge(resid.sem, resid.at(b))
                dve.tensor_tensor(stream[:, b], y_ps, stream[:, b], ALU.add).then_inc(finished.sem, 1)

            def set_up_columns():
                dve.wait_ge(s_attw, 32)
                prep(dve.tensor_copy(bq_rows[:, :], bcol[:, 0:1].to_broadcast([D, P])))
                prep(dve.tensor_copy(bv_rows[:, :], bcol[:, 2:3].to_broadcast([D, P])))
                dve.wait_ge(s_wt_ps, 1)
                dve.tensor_copy(wT[:, :, :, :], bM[0:D, 0:3 * D].rearrange("d (t i) -> d t i", t=3).unsqueeze(2)
                                .to_broadcast([D, 3, 2, D])).then_inc(s_wt, 1)

            def set_up_attention():
                dve.wait_ge(s_ab_ps, 1)
                prep(dve.tensor_scalar(a_hi[:, :], bG[:, 0:P], SCALE, None, ALU.mult))
                prep(dve.tensor_scalar(c_col[:, :], bG[:, P:P + 1], SCALE, None, ALU.mult))
                wv, vb = bG[:, 2 * P:2 * P + D + 1], bG[:, 3 * P:3 * P + D + 1]
                prep(dve.tensor_copy(wv_f[:, 0:D], wv[:, 0:D]))
                prep(dve.tensor_scalar(wv_f[:, D:D + 1], wv[:, D:D + 1], SCALE, None, ALU.mult))
                prep(dve.memset(wv_f[:, D + 1:VW], 0.0))
                prepared(PREP_AHI)
                prep(dve.scalar_tensor_tensor(out=a_lo[:, :], in0=bG[:, 0:P], scalar=SCALE,
                                              in1=a_hi[:, :].bitcast(F32), op0=ALU.mult, op1=ALU.subtract))
                prepared(PREP_WPAD)
                prep(dve.tensor_copy(wv_hi[:, :], wv_f[:, :]))
                dve.wait_ge(s_wp, 32)
                prep(dve.tensor_tensor(v_bias[:, 0:D], vb[:, 0:D], bp[:, :], ALU.add))
                prep(dve.tensor_scalar(v_bias[:, D:D + 1], vb[:, D:D + 1], SCALE, None, ALU.mult))
                prep(dve.memset(v_bias[:, D + 1:VW], 0.0))
                prepared(PREP_WVHI)
                prep(dve.tensor_tensor(wv_lo[:, :], wv_f[:, :], wv_hi[:, :].bitcast(F32), ALU.subtract))

            def set_up_experts():
                dve.wait_ge(s_moew, 16 * 15)
                prep(dve.tensor_copy(r_hi[:, :], r_f[:, :]))
                prep(dve.tensor_copy(b2_part[:, 0, :], b2_f[:, :]))
                dve.wait_ge(s_w1hi, 1)
                prep(dve.tensor_tensor(w1_lo[:, :], w1_f[:, :], w1_hi[:, :].bitcast(F32), ALU.subtract))
                prepared(PREP_B2)
                prep(dve.tensor_tensor(r_lo[:, :], r_f[:, :], r_hi[:, :].bitcast(F32), ALU.subtract))
                prep(dve.tensor_tensor(b2_rest[:, 0, :], b2_f[:, :], b2_part[:, 0, :], ALU.subtract))
                prepared(PREP_B2 + 3)
                prep(dve.tensor_copy(b2_part[:, 1, :], b2_rest[:, 0, :]))
                prepared(PREP_B2 + 4)
                prep(dve.tensor_tensor(b2_rest[:, 1, :], b2_rest[:, 0, :], b2_part[:, 1, :], ALU.subtract))
                prepared(PREP_B2 + 5)
                prep(dve.tensor_copy(b2_part[:, 2, :], b2_rest[:, 1, :]))
                prepared(PREP_B2 + 6)
                for n in range(SPLIT):
                    rows_n = slice(n * KG, n * KG + KG)
                    prep(dve.tensor_copy(b2_rows[rows_n, :], b2_part[rows_n, n, :]))

            def run(steps_, n=1):
                for _ in range(n):
                    next(steps_, None)

            def body(i):
                norm1 = norm_steps(0, i + 1) if has(i + 1) else iter(())
                norm2 = norm_steps(1, i) if has(i) else iter(())
                routing = route_steps(i - 1) if has(i - 1) else iter(())
                if has(i):
                    maximum(i, 0)
                    maximum(i, 1)
                    set_shift(i, 0)
                if has(i - 1):
                    normalise(1, i - 1)
                if has(i):
                    set_shift(i, 1)
                run(norm1, 2)
                if has(i):
                    maximum(i, 2)
                run(norm1)
                if has(i - 2):
                    scale_pair(i - 2, 2)
                run(norm1)
                if has(i):
                    set_shift(i, 2)
                run(norm1)
                if has(i):
                    maximum(i, 3)
                    set_shift(i, 3)
                if has(i - 2):
                    scale_pair(i - 2, 3)
                if has(i + 1):
                    normalise(0, i + 1)
                run(routing, 13)
                if has(i):
                    add_attention(i)
                if has(i - 1):
                    keep_weights(i - 1)
                run(norm2, 2)
                if has(i + 1):
                    g_low(i + 1)
                run(norm2)
                if has(i - 1):
                    scale_pair(i - 1, 0)
                run(norm2)
                if has(i - 1):
                    scale_pair(i - 1, 1)
                run(norm2)
                if has(i - 2):
                    finish(i - 2)
                if has(i + 1):
                    values(i + 1)

            set_up_columns()
            run(norm_steps(0, 0), 5)
            set_up_attention()
            normalise(0, 0)
            set_up_experts()
            dve.wait_ge(s_zeroed, 2)
            g_low(0)
            values(0)

            def tail(x, y):
                routing = route_steps(y)
                normalise(1, y)
                scale_pair(x, 2)
                scale_pair(x, 3)
                run(routing, 13)
                keep_weights(y)
                finish(x)
                scale_pair(y, 0)
                scale_pair(y, 1)
                scale_pair(y, 2)
                scale_pair(y, 3)
                finish(y)

            pipeline(dve, body, tail)


def constants():
    f = np.zeros((P, C_F32), np.float32)
    f[:, C_ID:C_ID + P] = np.eye(P)
    d = np.arange(D)
    exponent = (d - d % 2).astype(np.float32) / np.float32(D)
    inv_freq = np.power(np.float32(10000.0), -exponent)
    angle = np.arange(T, dtype=np.float32)[:, None] * inv_freq
    table = np.where(d % 2 == 0, np.sin(angle), np.cos(angle)).astype(np.float32)
    f[:, C_PE:C_PE + Q * D] = table.reshape(Q, P, D).transpose(1, 0, 2).reshape(P, Q * D)
    f[:, C_IOTA:C_IOTA + E] = np.arange(E)
    b = np.zeros((P, C_BF16), np.float32)
    b[:, C_ID:C_ID + P] = np.eye(P)
    b[:, C_MASK:C_MASK + P] = np.where(np.arange(P)[None, :] > np.arange(P)[:, None], MASKED, 0.0)
    for a in range(PAIRS):
        for part in range(SPLIT):
            for e in range(2):
                at = C_SEL + a * P + e * D
                b[part * E + 2 * a + e, at:at + D] = 1.0
    return f, b


def kernel(x, L0_tok_W, L0_attn_W_qkv, L0_attn_b_qkv, L0_attn_W_proj, L0_attn_b_proj, L0_ffn_router_w,
           L0_ffn_w1, L0_ffn_b1, L0_ffn_w2, L0_ffn_b2):
    import concourse.bacc as bacc
    from concourse.bass_utils import run_bass_kernel_spmd as run

    f, b = constants()
    arrays = {
        "ids": np.ascontiguousarray(np.asarray(x).reshape(B * Q, P).T),
        "table": L0_tok_W, "w_qkv": L0_attn_W_qkv,
        "b_qkv": np.asarray(L0_attn_b_qkv).reshape(3, D).T, "w_proj": L0_attn_W_proj,
        "b_proj": L0_attn_b_proj, "router": np.asarray(L0_ffn_router_w).T,
        "w1": L0_ffn_w1, "b1": np.asarray(L0_ffn_b1).reshape(PAIRS, P).T,
        "w2": L0_ffn_w2, "b2": L0_ffn_b2, "const": f, "const_b": b,
    }
    arrays = {name: np.ascontiguousarray(a) for name, a in arrays.items()}
    nc = bacc.Bacc("TRN2", target_bir_lowering=False, num_devices=1)
    aps = {name: nc.dram_tensor(name, a.shape, mybir.dt.from_np(a.dtype), kind="ExternalInput").ap()
           for name, a in arrays.items()}
    out = nc.dram_tensor("out", (B, T, D), F32, kind="ExternalOutput").ap()
    build(nc, **aps, out=out)
    return run(nc, [arrays], core_ids=[0]).results[0]["out"]
```
